# Optimizing a Trainium2 kernel written in Bass

```python
import numpy as np
import jax
import jax.numpy as jnp

def _softmax(x, axis=-1):
    return jax.nn.softmax(x, axis=axis)

def _gelu(x):
    return jax.nn.gelu(x, approximate=True)

def _silu(x):
    return jax.nn.silu(x)

def _sigmoid(x):
    return jax.nn.sigmoid(x)

def _layernorm(x, axis=-1, eps=1e-05):
    m = jnp.mean(x, axis=axis, keepdims=True)
    v = jnp.var(x, axis=axis, keepdims=True)
    return (x - m) / jnp.sqrt(v + eps)

def _scatter_add(tgt, idx, src, axis=0):
    return tgt.at[idx].add(src)

def _segment_sum(src, seg, n):
    return jax.ops.segment_sum(src, seg, n)
kernel_name = 'mk_gnn_resnorm_d4_gnn_r32_6ebc0c'

def setup_inputs(seed: int=0):
    np.random.seed(seed)
    _w = jnp.asarray

    def _rec_inputs():
        import jax
        import jax.numpy as jnp
        _gk = jax.random.key(seed)
        x = -8.776e-05 + 1 * jax.random.normal(jax.random.fold_in(_gk, 1), (50000, 128), jnp.float32)
        _s = jax.random.randint(jax.random.fold_in(_gk, 2), (25000,), 0, 50000, jnp.int32)
        _d = jax.random.randint(jax.random.fold_in(_gk, 3), (25000,), 0, 50000, jnp.int32)
        _loop = jnp.arange(50000, dtype=jnp.int32)
        src = jnp.concatenate([_s, _d, _loop])
        dst = jnp.concatenate([_d, _s, _loop])
        _o = jnp.argsort(dst, stable=True)
        src = src[_o]
        dst = dst[_o]
        return (x, src, dst)
    x, src, dst = _rec_inputs()

    def _L0_gnn_setup():
        import jax, jax.numpy as jnp
        import numpy as np
        N_NODES = 1250
        N_EDGES = 20000
        D_IN = 128
        D_OUT = 128
        key = jax.random.key(seed)
        k_h, k_src, k_dst, k_w = jax.random.split(key, 4)
        h = jax.random.normal(k_h, (N_NODES, D_IN), dtype=jnp.float32)
        src = jax.random.randint(k_src, (N_EDGES,), 0, N_NODES, dtype=jnp.int64)
        dst = jax.random.randint(k_dst, (N_EDGES,), 0, N_NODES, dtype=jnp.int64)
        kernel = jax.random.normal(k_w, (D_IN, D_OUT), dtype=jnp.float32) * (1.0 / np.sqrt(D_IN))
        bias = jnp.zeros((D_OUT,), dtype=jnp.float32)
        return {'h': h, 'src': src, 'dst': dst, 'kernel': kernel, 'bias': bias}
    _L0_gnn_all = _L0_gnn_setup()
    _L0_gnn_in = {k: v for k, v in _L0_gnn_all.items() if k in ('kernel', 'bias')}
    del _L0_gnn_all

    def _L1_gnn_setup():
        import jax, jax.numpy as jnp
        import numpy as np
        N = 50000
        E = 25000
        D = 128
        O = 128
        key = jax.random.key(seed)
        ks = jax.random.split(key, 12)
        s = 0.05
        inp = {'x': jax.random.normal(ks[0], (N, D), dtype=jnp.float32), 'edge_index': jax.random.randint(ks[1], (2, E), 0, N, dtype=jnp.int64), 'w_s2d': jax.random.normal(ks[2], (D, O), dtype=jnp.float32) * s, 'b_s2d': jnp.zeros((O,), dtype=jnp.float32), 'w_d2s': jax.random.normal(ks[3], (D, O), dtype=jnp.float32) * s, 'b_d2s': jnp.zeros((O,), dtype=jnp.float32), 'w_e1': jax.random.normal(ks[4], (2 * D, D), dtype=jnp.float32) * s, 'b_e1': jnp.zeros((D,), dtype=jnp.float32), 'w_e2': jax.random.normal(ks[5], (D, 1), dtype=jnp.float32) * s, 'b_e2': jnp.zeros((1,), dtype=jnp.float32), 'w_g1': jax.random.normal(ks[6], (2 * O, O), dtype=jnp.float32) * s, 'b_g1': jnp.zeros((O,), dtype=jnp.float32), 'w_g2': jax.random.normal(ks[7], (O, 1), dtype=jnp.float32) * s, 'b_g2': jnp.zeros((1,), dtype=jnp.float32)}
        return inp
    _L1_gnn_all = _L1_gnn_setup()
    _L1_gnn_in = {k: v for k, v in _L1_gnn_all.items() if k in ('w_s2d', 'b_s2d', 'w_d2s', 'b_d2s', 'w_e1', 'b_e1', 'w_e2', 'b_e2', 'w_g1', 'b_g1', 'w_g2', 'b_g2')}
    del _L1_gnn_all

    def _L2_gnn_setup():
        import jax, jax.numpy as jnp
        import numpy as np
        N_NODES = 10000
        N_EDGES = 20000
        DIM = 128

        def _sage_conv(h, src, dst, lw, lb, rw, n_nodes):
            msg = h[src]
            summed = jax.ops.segment_sum(msg, dst, num_segments=n_nodes)
            cnt = jax.ops.segment_sum(jnp.ones_like(dst, dtype=h.dtype), dst, num_segments=n_nodes)
            agg = summed / jnp.maximum(cnt, 1.0)[:, None]
            return agg @ lw.T + lb + h @ rw.T
        key = jax.random.key(seed)
        ks = jax.random.split(key, 10)
        s = 1.0 / np.sqrt(DIM)
        return {'x': jax.random.normal(ks[0], (N_NODES, DIM), dtype=jnp.float32), 'edge_index': jax.random.randint(ks[1], (2, N_EDGES), 0, N_NODES, dtype=jnp.int64), 'fc_w': jax.random.normal(ks[2], (DIM, DIM), dtype=jnp.float32) * s, 'fc_b': jax.random.normal(ks[3], (DIM,), dtype=jnp.float32) * s, 'f_lw': jax.random.normal(ks[4], (DIM, DIM), dtype=jnp.float32) * s, 'f_lb': jax.random.normal(ks[5], (DIM,), dtype=jnp.float32) * s, 'f_rw': jax.random.normal(ks[6], (DIM, DIM), dtype=jnp.float32) * s, 'n_lw': jax.random.normal(ks[7], (DIM, DIM), dtype=jnp.float32) * s, 'n_lb': jax.random.normal(ks[8], (DIM,), dtype=jnp.float32) * s, 'n_rw': jax.random.normal(ks[9], (DIM, DIM), dtype=jnp.float32) * s}
    _L2_gnn_all = _L2_gnn_setup()
    _L2_gnn_in = {k: v for k, v in _L2_gnn_all.items() if k in ('fc_w', 'fc_b', 'f_lw', 'f_lb', 'f_rw', 'n_lw', 'n_lb', 'n_rw')}
    del _L2_gnn_all

    def _L3_gnn_setup():
        import jax, jax.numpy as jnp
        import numpy as np
        N, E = (50000, 25000)
        IN_DIM, HID, HEADS, OUT_DIM = (128, 64, 4, 128)
        NEG_SLOPE = 0.2

        def _gat_forward(x, edge_index, W, att_src, att_dst, bias, fc_w, fc_b):
            n = x.shape[0]
            h = (x @ W).reshape(n, HEADS, HID)
            loops = jnp.arange(n, dtype=edge_index.dtype)
            src = jnp.concatenate([edge_index[0], loops])
            dst = jnp.concatenate([edge_index[1], loops])
            a_src = jnp.einsum('nhf,hf->nh', h, att_src)
            a_dst = jnp.einsum('nhf,hf->nh', h, att_dst)
            e = jax.nn.leaky_relu(a_src[src] + a_dst[dst], NEG_SLOPE)
            m = jax.ops.segment_max(e, dst, num_segments=n)
            ex = jnp.exp(e - m[dst])
            denom = jax.ops.segment_sum(ex, dst, num_segments=n)
            alpha = ex / denom[dst]
            msg = h[src] * alpha[:, :, None]
            agg = jax.ops.segment_sum(msg, dst, num_segments=n)
            out = agg.reshape(n, HEADS * HID) + bias
            out = jax.nn.relu(out)
            return out @ fc_w + fc_b
        key = jax.random.key(seed)
        ks = jax.random.split(key, 8)
        s = 1.0 / np.sqrt(IN_DIM)
        x = jax.random.normal(ks[0], (N, IN_DIM), dtype=jnp.float32)
        edge_index = jax.random.randint(ks[1], (2, E), 0, N, dtype=jnp.int64)
        W = jax.random.uniform(ks[2], (IN_DIM, HEADS * HID), jnp.float32, -s, s)
        att_src = jax.random.uniform(ks[3], (HEADS, HID), jnp.float32, -s, s)
        att_dst = jax.random.uniform(ks[4], (HEADS, HID), jnp.float32, -s, s)
        bias = jnp.zeros((HEADS * HID,), jnp.float32)
        sf = 1.0 / np.sqrt(HEADS * HID)
        fc_w = jax.random.uniform(ks[5], (HEADS * HID, OUT_DIM), jnp.float32, -sf, sf)
        fc_b = jax.random.uniform(ks[6], (OUT_DIM,), jnp.float32, -sf, sf)
        return {'x': x, 'edge_index': edge_index, 'W': W, 'att_src': att_src, 'att_dst': att_dst, 'bias': bias, 'fc_w': fc_w, 'fc_b': fc_b}
    _L3_gnn_all = _L3_gnn_setup()
    _L3_gnn_in = {k: v for k, v in _L3_gnn_all.items() if k in ('W', 'att_src', 'att_dst', 'bias', 'fc_w', 'fc_b')}
    del _L3_gnn_all
    return {'x': x, 'src': src, 'dst': dst, 'L0_gnn_kernel': _L0_gnn_in['kernel'], 'L0_gnn_bias': _L0_gnn_in['bias'], 'L1_gnn_w_s2d': _L1_gnn_in['w_s2d'], 'L1_gnn_b_s2d': _L1_gnn_in['b_s2d'], 'L1_gnn_w_d2s': _L1_gnn_in['w_d2s'], 'L1_gnn_b_d2s': _L1_gnn_in['b_d2s'], 'L1_gnn_w_e1': _L1_gnn_in['w_e1'], 'L1_gnn_b_e1': _L1_gnn_in['b_e1'], 'L1_gnn_w_e2': _L1_gnn_in['w_e2'], 'L1_gnn_b_e2': _L1_gnn_in['b_e2'], 'L1_gnn_w_g1': _L1_gnn_in['w_g1'], 'L1_gnn_b_g1': _L1_gnn_in['b_g1'], 'L1_gnn_w_g2': _L1_gnn_in['w_g2'], 'L1_gnn_b_g2': _L1_gnn_in['b_g2'], 'L2_gnn_fc_w': _L2_gnn_in['fc_w'], 'L2_gnn_fc_b': _L2_gnn_in['fc_b'], 'L2_gnn_f_lw': _L2_gnn_in['f_lw'], 'L2_gnn_f_lb': _L2_gnn_in['f_lb'], 'L2_gnn_f_rw': _L2_gnn_in['f_rw'], 'L2_gnn_n_lw': _L2_gnn_in['n_lw'], 'L2_gnn_n_lb': _L2_gnn_in['n_lb'], 'L2_gnn_n_rw': _L2_gnn_in['n_rw'], 'L3_gnn_W': _L3_gnn_in['W'], 'L3_gnn_att_src': _L3_gnn_in['att_src'], 'L3_gnn_att_dst': _L3_gnn_in['att_dst'], 'L3_gnn_bias': _L3_gnn_in['bias'], 'L3_gnn_fc_w': _L3_gnn_in['fc_w'], 'L3_gnn_fc_b': _L3_gnn_in['fc_b']}

def reference(x, src, dst, L0_gnn_kernel, L0_gnn_bias, L1_gnn_w_s2d, L1_gnn_b_s2d, L1_gnn_w_d2s, L1_gnn_b_d2s, L1_gnn_w_e1, L1_gnn_b_e1, L1_gnn_w_e2, L1_gnn_b_e2, L1_gnn_w_g1, L1_gnn_b_g1, L1_gnn_w_g2, L1_gnn_b_g2, L2_gnn_fc_w, L2_gnn_fc_b, L2_gnn_f_lw, L2_gnn_f_lb, L2_gnn_f_rw, L2_gnn_n_lw, L2_gnn_n_lb, L2_gnn_n_rw, L3_gnn_W, L3_gnn_att_src, L3_gnn_att_dst, L3_gnn_bias, L3_gnn_fc_w, L3_gnn_fc_b):
    import jax
    import jax.numpy as jnp

    def _L0_gnn_ref(h, src, dst, kernel, bias):
        import jax, jax.numpy as jnp
        import numpy as np
        N_NODES = 1250
        N_EDGES = 20000
        D_IN = 128
        D_OUT = 128
        n = h.shape[0]
        msgs = h[src]
        agg = jax.ops.segment_sum(msgs, dst, num_segments=n)
        deg = jax.ops.segment_sum(jnp.ones((src.shape[0],), h.dtype), src, num_segments=n)
        norm = (deg ** (-0.5))[:, None]
        return jax.nn.relu(agg @ kernel * norm + bias)

    def _L1_gnn_ref(x, edge_index, w_s2d, b_s2d, w_d2s, b_d2s, w_e1, b_e1, w_e2, b_e2, w_g1, b_g1, w_g2, b_g2):
        import jax, jax.numpy as jnp
        import numpy as np
        N = 50000
        E = 25000
        D = 128
        O = 128
        num_nodes = x.shape[0]
        src = edge_index[0]
        dst = edge_index[1]
        x_src = x[src]
        x_dst = x[dst]
        edge_input = jnp.concatenate([x_src, x_dst], axis=-1)
        h_e = jax.nn.relu(edge_input @ w_e1 + b_e1)
        edge_score = jax.nn.sigmoid((h_e @ w_e2 + b_e2)[:, 0])
        msg_in = (x_src @ w_s2d + b_s2d) * edge_score[:, None]
        msg_out = (x_dst @ w_d2s + b_d2s) * edge_score[:, None]
        h_in = jax.ops.segment_sum(msg_in, dst, num_segments=num_nodes)
        h_out = jax.ops.segment_sum(msg_out, src, num_segments=num_nodes)
        ones = jnp.ones((src.shape[0],), dtype=x.dtype)
        in_deg = jnp.maximum(jax.ops.segment_sum(ones, dst, num_segments=num_nodes), 1.0)
        out_deg = jnp.maximum(jax.ops.segment_sum(ones, src, num_segments=num_nodes), 1.0)
        h_in = h_in / in_deg[:, None]
        h_out = h_out / out_deg[:, None]
        gate_input = jnp.concatenate([h_in, h_out], axis=-1)
        h_g = jax.nn.relu(gate_input @ w_g1 + b_g1)
        g = jax.nn.sigmoid(h_g @ w_g2 + b_g2)
        fused = g * h_in + (1.0 - g) * h_out
        return fused + x

    def _L2_gnn_ref(x, edge_index, fc_w, fc_b, f_lw, f_lb, f_rw, n_lw, n_lb, n_rw):
        import jax, jax.numpy as jnp
        import numpy as np
        N_NODES = 10000
        N_EDGES = 20000
        DIM = 128

        def _sage_conv(h, src, dst, lw, lb, rw, n_nodes):
            msg = h[src]
            summed = jax.ops.segment_sum(msg, dst, num_segments=n_nodes)
            cnt = jax.ops.segment_sum(jnp.ones_like(dst, dtype=h.dtype), dst, num_segments=n_nodes)
            agg = summed / jnp.maximum(cnt, 1.0)[:, None]
            return agg @ lw.T + lb + h @ rw.T
        n_nodes = x.shape[0]
        src, dst = (edge_index[0], edge_index[1])
        inp = x @ fc_w.T + fc_b
        h = jax.nn.relu(_sage_conv(x, src, dst, f_lw, f_lb, f_rw, n_nodes))
        h = _sage_conv(h, src, dst, n_lw, n_lb, n_rw, n_nodes)
        return jax.nn.relu(h + inp)

    def _L3_gnn_ref(x, edge_index, W, att_src, att_dst, bias, fc_w, fc_b):
        import jax, jax.numpy as jnp
        import numpy as np
        N, E = (50000, 25000)
        IN_DIM, HID, HEADS, OUT_DIM = (128, 64, 4, 128)
        NEG_SLOPE = 0.2

        def _gat_forward(x, edge_index, W, att_src, att_dst, bias, fc_w, fc_b):
            n = x.shape[0]
            h = (x @ W).reshape(n, HEADS, HID)
            loops = jnp.arange(n, dtype=edge_index.dtype)
            src = jnp.concatenate([edge_index[0], loops])
            dst = jnp.concatenate([edge_index[1], loops])
            a_src = jnp.einsum('nhf,hf->nh', h, att_src)
            a_dst = jnp.einsum('nhf,hf->nh', h, att_dst)
            e = jax.nn.leaky_relu(a_src[src] + a_dst[dst], NEG_SLOPE)
            m = jax.ops.segment_max(e, dst, num_segments=n)
            ex = jnp.exp(e - m[dst])
            denom = jax.ops.segment_sum(ex, dst, num_segments=n)
            alpha = ex / denom[dst]
            msg = h[src] * alpha[:, :, None]
            agg = jax.ops.segment_sum(msg, dst, num_segments=n)
            out = agg.reshape(n, HEADS * HID) + bias
            out = jax.nn.relu(out)
            return out @ fc_w + fc_b
        return _gat_forward(x, edge_index, W, att_src, att_dst, bias, fc_w, fc_b)
    edge_index = jnp.stack([src, dst])
    x = _layernorm(x + _L0_gnn_ref(x, src, dst, L0_gnn_kernel, L0_gnn_bias), axis=-1)
    x = _layernorm(x + _L1_gnn_ref(x, edge_index, L1_gnn_w_s2d, L1_gnn_b_s2d, L1_gnn_w_d2s, L1_gnn_b_d2s, L1_gnn_w_e1, L1_gnn_b_e1, L1_gnn_w_e2, L1_gnn_b_e2, L1_gnn_w_g1, L1_gnn_b_g1, L1_gnn_w_g2, L1_gnn_b_g2), axis=-1)
    x = _layernorm(x + _L2_gnn_ref(x, edge_index, L2_gnn_fc_w, L2_gnn_fc_b, L2_gnn_f_lw, L2_gnn_f_lb, L2_gnn_f_rw, L2_gnn_n_lw, L2_gnn_n_lb, L2_gnn_n_rw), axis=-1)
    x = _layernorm(x + _L3_gnn_ref(x, edge_index, L3_gnn_W, L3_gnn_att_src, L3_gnn_att_dst, L3_gnn_bias, L3_gnn_fc_w, L3_gnn_fc_b), axis=-1)
    return x

_drawn_inputs = setup_inputs


def setup_inputs(seed=0):
    import zlib

    import numpy as np

    out = dict(_drawn_inputs(seed))
    spreads = {'L0_gnn_bias': (0.0, 0.1),
     'L1_gnn_b_s2d': (0.0, 0.601),
     'L1_gnn_b_d2s': (0.0, 0.466),
     'L1_gnn_b_e1': (0.0, 0.8),
     'L1_gnn_b_g1': (0.0, 2.0),
     'L3_gnn_bias': (0.0, 0.1)}
    factors = {'L1_gnn_w_e1': 4.891,
     'L1_gnn_w_e2': 4.457,
     'L1_gnn_w_g1': 8.0,
     'L1_gnn_w_g2': 8.0,
     'L3_gnn_att_src': 7.469,
     'L3_gnn_att_dst': 23.927}
    for name, (base, spread) in spreads.items():
        noise = np.random.default_rng([zlib.crc32(name.encode()), seed]).standard_normal(out[name].shape)
        drawn = base * np.exp(spread * noise) if base else spread * noise
        out[name] = jnp.asarray(drawn.astype(out[name].dtype))
    for name, factor in factors.items():
        out[name] = (out[name] * factor).astype(out[name].dtype)
    return out
```

```python
import concourse.bass as bass
from concourse import mybir
from contextlib import ExitStack

FP32 = mybir.dt.float32
BF16 = mybir.dt.bfloat16
FP16 = mybir.dt.float16
I32 = mybir.dt.int32
ALU = mybir.AluOpType
ACT = mybir.ActivationFunctionType
AX = mybir.AxisListType

P = 128
D = 128
W = 112
G = 3
HEADS, HID = 4, 64
HF = HEADS * HID
HILO = 22
RING = 16
NRING = 8
QUAD = 4
ROUTE = {"to_win": (0, 32), "of_win": (64, 96)}
AR = 8
SH = 4
ROUND = 12582912.0
BIG = 1.0e30
EPS = 1e-5
SLOPE = 0.2


class Shapes:

    def __init__(self, nodes, edges):
        self.n, self.e = nodes, edges
        self.nw = -(-(-(-nodes // W)) // G) * G
        self.ng = self.nw // G
        self.npad = self.nw * W
        self.q = -(-edges // P)
        self.nt = -(-self.q // RING) * RING
        self.ns = -(-(edges // P + self.nw) // RING) * RING
        self.na = min(self.ns, -(-(self.nw + self.nw // 10) // RING) * RING)
        self.hi = -(-self.nw // HILO)
        self.nb = self.hi * HILO
        self.dump = self.nw + 1
        self.rows = (self.nw + 1 + RING) * W


def wait(eng, sem, value):
    if not isinstance(value, int) or value > 0:
        eng.wait_ge(sem, value)


def wait_then_step(eng, sem, value, step):
    if not isinstance(value, int) or value > 0:
        eng.wait_ge(sem, value)
        eng.sem_inc(step, 1)


def steps(eng, stages, lo, hi, ring, peel_last=0):
    longest = max(lag for lag, _ in stages)
    head = -(-(longest + (ring if lo == 0 else 0)) // ring) * ring
    for s in range(lo, min(lo + head, hi)):
        for lag, f in stages:
            if s - lag >= lo:
                f(s // ring, s % ring - lag)
    first = (lo + head) // ring
    full = max(first, (hi - peel_last) // ring)
    if full > first:
        with eng.Fori(first, full) as i:
            for u in range(ring):
                for lag, f in stages:
                    f(i, u - lag)
    for s in range(min(full * ring, hi), hi + longest):
        for lag, f in stages:
            if lo <= s - lag < hi:
                f(full, s - lag - full * ring)


def fix(i, c, ring):
    return i * ring + c


class Sems:

    def __init__(self, nc, tag):
        self.nc, self.tag, self.all = nc, tag, []

    def __call__(self, name, n=None):
        if n is not None:
            return [self(f"{name}{k}") for k in range(n)]
        s = self.nc.alloc_semaphore(f"{self.tag}_{name}")
        self.all.append(s)
        return s

    def close(self):
        self.nc.clear_and_free_semaphores(self.all)
        self.nc.all_engine_barrier()


def row(vector):
    return vector.rearrange("(a n) -> a n", a=1)


class Chain:

    def __init__(self, eng, sem):
        self.eng, self.sem, self.n = eng, sem, 0

    def __call__(self, ins):
        self.n += 1
        ins.then_inc(self.sem, 1)
        self.eng.wait_ge(self.sem, self.n)


def load_and_count(nc, z, src, dst, t, wts, dram):
    sems = Sems(nc, "count")
    edges_in, consts, weights_in = sems("edges_in"), sems("consts"), sems("weights_in")
    hot, hot_used, counts, counts_sb, counts_out = sems("hot"), sems("hot_used"), sems("counts"), sems("counts_sb"), sems("counts_out")
    split, chain, cleared = sems("split"), sems("chain"), sems("cleared")
    trans, trans_sb, mchain, init_out = sems("trans"), sems("trans_sb"), sems("mchain"), sems("init_out")
    ctx = ExitStack()
    sb = lambda name, shape, dt: ctx.enter_context(nc.sbuf_tensor(name, shape, dt))
    NT = z.nt
    raw = sb("raw_edges", [P, 2, NT], I32)
    val = sb("edge_ends", [P, 2, NT], FP32)
    tmp = sb("edge_tmp", [P, 2, NT], FP32)
    hi = sb("hi", [P, 2, NT], FP32)
    lw = sb("lw", [P, 2, NT], FP32)
    iota_hi = sb("iota_hi", [P, HILO], FP32)
    hot_hi = sb("hot_hi", [P, 2, 2, 8, HILO], BF16)
    hot_lo = sb("hot_lo", [P, 2, 2, 8, HILO], BF16)
    zeros = sb("zeros_bf", [P, HILO], BF16)
    cnt_sb = sb("cnt_sb", [z.hi, 2, HILO], FP32)
    fill = sb("fill", [P, z.ns, 2], I32)
    ps_cnt = [ctx.enter_context(nc.psum_tensor(f"ps_cnt{k}", [HILO, 512], FP32)) for k in range(2)]
    ps_w = [ctx.enter_context(nc.psum_tensor(f"ps_w{k}", [P, 4, P], FP32)) for k in range(2)]
    mats = [wts[k] for k in ("L2_fc_w", "L2_f_lw", "L2_f_rw", "L2_n_lw", "L2_n_rw")]
    mats_t = [wts[k + "T"] for k in ("L2_fc_w", "L2_f_lw", "L2_f_rw", "L2_n_lw", "L2_n_rw")]
    full, rest = z.e // z.q, z.e % z.q
    n_weights = len(wts["loads"])
    with nc.Block() as block:
        @block.sync
        def _(sp):
            sp.wait_ge(cleared, 1)
            for k, v in enumerate((dst, src)):
                sp.dma_start(raw[0:full, k, 0:z.q], v[0:full * z.q].rearrange("(p q) -> p q", q=z.q)).then_inc(edges_in, 16)
                if rest:
                    sp.dma_start(raw[full:full + 1, k, 0:rest], row(v[full * z.q:z.e])).then_inc(edges_in, 16)
            for to, of in wts["loads"]:
                sp.dma_start(to, of, allow_slow_non_contiguous=of.shape[-1] == 1).then_inc(weights_in, 16)
            sp.wait_ge(consts, 9)
            for k in range(2):
                sp.dma_start(dram["slots"][k].rearrange("(p c) v -> p c v", p=P), fill[:, :, :]).then_inc(init_out, 16)
            sp.wait_ge(counts_sb, 2)
            for k in range(2):
                sp.dma_start(dram["counts"][k].rearrange("(h l) -> h l", l=HILO), cnt_sb[:, k, :]).then_inc(counts_out, 16)
            sp.wait_ge(counts_out, 32)
            sp.wait_ge(init_out, 32)

        @block.gpsimd
        def _(pool):
            pool.iota(t["iota_win"][:, :], [[1, z.nb]], base=0, channel_multiplier=0, allow_small_or_imprecise_dtypes=True).then_inc(consts, 1)
            pool.iota(t["iota_w"][:, :], [[1, W]], base=0, channel_multiplier=0, allow_small_or_imprecise_dtypes=True).then_inc(consts, 1)
            pool.iota(t["iota_wh"][:, :], [[1, W]], base=0, channel_multiplier=0, allow_small_or_imprecise_dtypes=True).then_inc(consts, 1)
            pool.iota(iota_hi[:, :], [[1, HILO]], base=0, channel_multiplier=0, allow_small_or_imprecise_dtypes=True).then_inc(consts, 1)
            pool.iota(fill[:, :, 0], [[0, z.ns]], base=0, channel_multiplier=z.n // P).then_inc(consts, 1)
            pool.memset(fill[:, :, 1], -1).then_inc(consts, 1)
            pool.memset(t["ident"][:, :], 0.0).then_inc(mchain, 1)
            pool.memset(t["before"][:, :], 1.0).then_inc(mchain, 1)
            pool.memset(t["after"][:, :], 1.0).then_inc(mchain, 1)
            pool.wait_ge(mchain, 3)
            pool.affine_select(out=t["ident"][:, :], in_=t["ident"][:, :], compare_op=ALU.not_equal, fill=1.0, base=0,
                               pattern=[[-1, P]], channel_multiplier=1).then_inc(consts, 1)
            pool.affine_select(out=t["before"][:, :], in_=t["before"][:, :], compare_op=ALU.is_gt, fill=0.0, base=0,
                               pattern=[[1, P]], channel_multiplier=-1).then_inc(consts, 1)
            pool.affine_select(out=t["after"][:, :], in_=t["after"][:, :], compare_op=ALU.is_ge, fill=0.0, base=0,
                               pattern=[[-1, P]], channel_multiplier=1).then_inc(consts, 1)

        @block.scalar
        def _(act):
            for k in range(5):
                act.wait_ge(trans, k + 1)
                act.activation(mats_t[k][:, :], ps_w[k % 2][:, 0, :], ACT.Copy).then_inc(trans_sb, 1)

        @block.tensor
        def _(pe):
            pe.wait_ge(weights_in, 16 * n_weights)
            pe.wait_ge(consts, 9)
            for k in range(5):
                if k >= 2:
                    pe.wait_ge(trans_sb, k - 1)
                pe.transpose(ps_w[k % 2][:, 0, :], mats[k][:, :], t["ident"][:, :]).then_inc(trans, 1)
            pe.wait_ge(cleared, 2)
            for k in range(2):
                pe.matmul(ps_cnt[k][0:z.hi, 0:HILO], zeros[:, 0:z.hi], zeros[:, :], start=True, stop=False)

            def count(i, c):
                pe.wait_ge(hot, fix(i, c, 2) + 1)
                for k in range(2):
                    for j in range(8):
                        ins = pe.matmul(ps_cnt[k][0:z.hi, 0:HILO], hot_hi[:, c % 2, k, j, 0:z.hi], hot_lo[:, c % 2, k, j, :],
                                        start=False, stop=False)
                ins.then_inc(hot_used, 1)
            steps(pe, [(0, count)], 0, NT // 8, 2)
            for k in range(2):
                ins = pe.matmul(ps_cnt[k][0:z.hi, 0:HILO], zeros[:, 0:z.hi], zeros[:, :], start=False, stop=True)
            ins.then_inc(counts, 1)

        @block.vector
        def _(dve):
            dve.memset(raw[:, :, :], -1).then_inc(cleared, 1)
            dve.memset(zeros[:, :], 0.0).then_inc(cleared, 1)
            ch = Chain(dve, chain)
            ch(dve.memset(t["ones"][:, :], 1.0))
            ch(dve.memset(t["ones_row"][:, :], 1.0))
            dve.wait_ge(edges_in, 32 * (2 if rest else 1))
            dve.wait_ge(consts, 6)
            ch(dve.tensor_copy(val[:, :, :], raw[:, :, :]))
            ch(dve.tensor_tensor(t["self_edge"][:, :], val[:, 0, :], val[:, 1, :], ALU.is_equal))
            ch(dve.tensor_scalar(t["other_edge"][:, :], t["self_edge"][:, :], -1.0, 1.0, ALU.mult, ALU.add))
            ch(dve.tensor_scalar(tmp[:, :, :], val[:, :, :], 0.5, 1.0 / W, ALU.add, ALU.mult))
            ch(dve.tensor_scalar(tmp[:, :, :], tmp[:, :, :], 0.5, None, ALU.subtract))
            ch(dve.tensor_scalar(tmp[:, :, :], tmp[:, :, :], ROUND, None, ALU.add))
            ch(dve.tensor_scalar(t["win"][:, :, :], tmp[:, :, :], ROUND, None, ALU.subtract))
            ch(dve.scalar_tensor_tensor(t["place"][:, :, :], t["win"][:, :, :], -float(W), val[:, :, :], ALU.mult, ALU.add))
            for k in range(2):
                ch(dve.tensor_copy(t["carry"][:, :, k, 0], val[:, 1 - k, :]))
                ch(dve.tensor_copy(t["carry"][:, :, k, 1], t["place"][:, k, :]))
            ch(dve.tensor_scalar(tmp[:, :, :], t["win"][:, :, :], 0.5, 1.0 / HILO, ALU.add, ALU.mult))
            ch(dve.tensor_scalar(tmp[:, :, :], tmp[:, :, :], 0.5, None, ALU.subtract))
            ch(dve.tensor_scalar(tmp[:, :, :], tmp[:, :, :], ROUND, None, ALU.add))
            ch(dve.tensor_scalar(hi[:, :, :], tmp[:, :, :], ROUND, None, ALU.subtract))
            ch(dve.scalar_tensor_tensor(lw[:, :, :], hi[:, :, :], -float(HILO), t["win"][:, :, :], ALU.mult, ALU.add))
            for k in range(2):
                ch(dve.scalar_tensor_tensor(hi[:, k, :], hi[:, k, :], 1.0, t["other_edge"][:, :], ALU.add, ALU.mult))
            ch(dve.tensor_scalar(hi[:, :, :], hi[:, :, :], 1.0, None, ALU.subtract))

            def one_hot(i, c):
                wait(dve, hot_used, fix(i, c, 2) - 1)
                shape = [P, 8, HILO]
                bc = iota_hi[:, :].unsqueeze(1).to_broadcast(shape)
                for k in range(2):
                    for to, of in ((hot_hi, hi), (hot_lo, lw)):
                        part = of[:, k, bass.ds(fix(i, c, 2) * 8, 8)]
                        ins = dve.tensor_tensor(to[:, c % 2, k, :, :], part.unsqueeze(2).to_broadcast(shape), bc, ALU.is_equal)
                        last = k == 1 and to is hot_lo
                        ins.then_inc(hot if last else split, 1)
            steps(dve, [(0, one_hot)], 0, NT // 8, 2)
            dve.wait_ge(counts, 1)
            for k in range(2):
                dve.tensor_copy(cnt_sb[:, k, :], ps_cnt[k][0:z.hi, 0:HILO]).then_inc(counts_sb, 1)
            dve.wait_ge(weights_in, 16 * n_weights)
            for n, name in enumerate(("L3_att_src", "L3_att_dst")):
                ch(dve.tensor_tensor(t["att_tmp"][:, :], wts["L3_W"][:, 0:HF], wts[name][:, :], ALU.mult))
                ch(dve.tensor_reduce(wts["L3_W"][:, HF + HEADS * n:HF + HEADS * (n + 1)],
                                     t["att_tmp"][:, :].rearrange("p (h f) -> p h f", h=HEADS), AX.X, ALU.add))
            ch(dve.tensor_tensor(wts["L2_bias"][:, :], wts["L2_fc_b"][:, :], wts["L2_n_lb"][:, :], ALU.add))
    ctx.close()
    sems.close()


def plan_slots(nc, z, t, dram):
    sems = Sems(nc, "plan")
    counts_in, ends_out, ends_in, chain = sems("counts_in"), sems("ends_out"), sems("ends_in"), sems("chain")
    col, over, over_sum, consts, rows_out, used = sems("col"), sems("over"), sems("over_sum"), sems("consts"), sems("rows_out"), sems("used")
    ctx = ExitStack()
    sb = lambda name, shape, dt: ctx.enter_context(nc.sbuf_tensor(name, shape, dt))
    NB, NS, Q = z.nb, z.ns, -(-z.nw // P)
    cnt = sb("cnt", [P, 2, NB], FP32)
    slots = sb("slots_of", [P, 2, NB], FP32)
    ends = sb("ends", [P, 2, NB], FP32)
    zero = sb("zero_nb", [P, P], FP32)
    ends_col = sb("ends_col", [P, 2, Q], FP32)
    iota_s = sb("iota_s", [P, NS + 2], FP32)
    spare = sb("spare", [P, NS], FP32)
    ge = sb("ge", [P, 2, NS + 2], BF16)
    win = sb("slot_win", [P, 2, NS + 2], FP32)
    last = sb("last", [P, NS], FP32)
    below = sb("below", [P, NS], FP32)
    total = sb("total", [1, 1], FP32)
    cuts = [(a, min(a + 512, NS + 2)) for a in range(0, NS + 2, 512)]
    ps = [[ctx.enter_context(nc.psum_tensor(f"ps_over{k}{j}", [P, 512], FP32)) for j in range(len(cuts))] for k in range(2)]
    with nc.Block() as block:
        @block.sync
        def _(sp):
            for k in range(2):
                sp.dma_start(cnt[:, k, :], dram["counts"][k].partition_broadcast(P)).then_inc(counts_in, 16)
            sp.wait_ge(chain, 11)
            for k in range(2):
                sp.dma_start(row(dram["ends"][k][0:z.nw]), ends[0:1, k, 0:z.nw]).then_inc(ends_out, 16)
                if Q * P > z.nw:
                    sp.dma_start(row(dram["ends"][k][z.nw:Q * P]), zero[0:1, 0:Q * P - z.nw]).then_inc(ends_out, 16)
            sp.wait_ge(ends_out, 32 * (2 if Q * P > z.nw else 1))
            with nc.allow_non_contiguous_dma("small transposing load"):
                for k in range(2):
                    sp.dma_start(ends_col[:, k, :], dram["ends"][k].rearrange("(q p) -> p q", p=P)).then_inc(ends_in, 16)
            sp.wait_ge(ends_in, 32)

        @block.gpsimd
        def _(pool):
            pool.iota(iota_s[:, :], [[1, NS + 2]], base=-1, channel_multiplier=0, allow_small_or_imprecise_dtypes=True).then_inc(consts, 1)
            pool.iota(spare[:, :].rearrange("p (a b) -> p a b", b=RING), [[0, NS // RING], [1, RING]], base=z.dump,
                      channel_multiplier=0, allow_small_or_imprecise_dtypes=True).then_inc(consts, 1)

        @block.tensor
        def _(pe):
            for q in range(Q):
                for k in range(2):
                    pe.wait_ge(over, 2 * q + k + 1)
                    for j, (a, b) in enumerate(cuts):
                        ins = pe.matmul(ps[k][j][:, 0:b - a], t["ones"][:, :], ge[:, k, a:b], start=(q == 0), stop=(q == Q - 1))
                    ins.then_inc(over_sum, 1)

        @block.vector
        def _(dve):
            ch = Chain(dve, chain)
            ch(dve.memset(zero[:, :], BIG))
            dve.wait_ge(counts_in, 32)
            ch(dve.tensor_scalar(slots[:, :, :], cnt[:, :, :], 1.0, P / 2.0 - 0.5, ALU.max, ALU.add))
            ch(dve.tensor_scalar(slots[:, :, :], slots[:, :, :], 1.0 / P, ROUND, ALU.mult, ALU.add))
            ch(dve.tensor_scalar(slots[:, :, :], slots[:, :, :], ROUND, None, ALU.subtract))
            ch(dve.memset(cnt[:, :, :], 0.0))
            for k in range(2):
                ch(dve.tensor_tensor_scan(ends[:, k, :], slots[:, k, :], cnt[:, k, :], 0.0, ALU.add, ALU.add))
            ch(dve.tensor_tensor(t["base"][:, :, :], ends[:, :, :], slots[:, :, :], ALU.subtract))
            ch(dve.tensor_scalar(t["base"][:, :, :], t["base"][:, :, :], float(P), None, ALU.mult))
            ch(dve.tensor_tensor(total[0:1, :], ends[0:1, 0, z.nw - 1:z.nw], ends[0:1, 1, z.nw - 1:z.nw], ALU.max))
            ch(dve.tensor_copy(t["total"][0:1, :], total[0:1, :]))
            assert ch.n == 11
            dve.wait_ge(ends_in, 32)
            dve.wait_ge(consts, 2)
            for q in range(Q):
                for k in range(2):
                    if q:
                        dve.wait_ge(over_sum, 2 * q - 1 + k)
                    dve.tensor_scalar(ge[:, k, :], iota_s[:, :], ends_col[:, k, q:q + 1], None, ALU.is_ge).then_inc(over, 1)
            dve.wait_ge(over_sum, 2 * Q)
            for k in range(2):
                for j, (a, b) in enumerate(cuts):
                    ch(dve.tensor_copy(win[:, k, a:b], ps[k][j][:, 0:b - a]))
                mid, lead, tail = win[:, k, 1:NS + 1], win[:, k, 0:NS], win[:, k, 2:NS + 2]
                ch(dve.tensor_tensor(t["keep"][:, k, :], mid, lead, ALU.is_equal))
                ch(dve.memset(t["keep"][:, k, 0:1], 0.0))
                if k == 0:
                    ch(dve.tensor_scalar(t["sink"][:, :], t["keep"][:, k, :], 1.0, BIG, ALU.subtract, ALU.mult))
                ch(dve.tensor_tensor(last[:, :], mid, tail, ALU.not_equal))
                ch(dve.tensor_scalar(below[:, :], mid, float(z.nw), None, ALU.is_lt))
                ch(dve.tensor_tensor(last[:, :], last[:, :], below[:, :], ALU.mult))
                ch(dve.tensor_tensor(below[:, :], mid, spare[:, :], ALU.subtract))
                ch(dve.tensor_tensor(below[:, :], below[:, :], last[:, :], ALU.mult))
                ch(dve.tensor_tensor(below[:, :], below[:, :], spare[:, :], ALU.add))
                a = ROUTE["to_win"][k]
                ch(dve.tensor_copy(t["route"][a:a + 1, :], below[a:a + 1, :]))
                ch(dve.tensor_scalar(last[:, :], mid, float(z.nw - 1), None, ALU.min))
                a = ROUTE["of_win"][k]
                ch(dve.tensor_copy(t["route"][a:a + 1, :], last[a:a + 1, :]))
    ctx.close()
    sems.close()


def sort_edges(nc, z, t, dram):
    sems = Sems(nc, "sort")
    masks, hot, lohot, rank, base_in, used, taken = (sems(n) for n in ("masks", "hot", "lohot", "rank", "base_in", "used", "taken"))
    place, place_chain, carried, counted, sent_done, step = (sems(n) for n in ("place", "place_chain", "carried", "counted", "done", "step"))
    counts_sb, ids = sems("counts_sb"), sems("ids")
    sent = sems("sent", RING)
    ctx = ExitStack()
    sb = lambda name, shape, dt: ctx.enter_context(nc.sbuf_tensor(name, shape, dt))
    NW, NT, NS = z.nw, z.nt, z.ns
    NE = -(-NW // 4) * 4
    M = 4
    before = sb("before_r", [P, M, P], BF16)
    after = sb("after_r", [P, M, P], BF16)
    hotw = sb("hotw", [P, M, 2, NE], BF16)
    hotp = sb("hotp", [P, M, 3, W], BF16)
    junk = sb("junk", [P, 2, NW], FP32)
    pos = sb("pos", [P, RING, 2], FP32)
    quo = sb("quo", [P, 8, 2], FP32)
    rem = sb("rem", [P, 8, 2], FP32)
    idx = sb("idx", [P, RING, 2], I32)
    carry = sb("carry_r", [P, RING, 2, 2], I32)
    zeros = sb("zeros_w", [P, max(NW, P)], BF16)
    ps_rank = [ctx.enter_context(nc.psum_tensor(f"ps_rank{k}", [P, 512], FP32)) for k in range(2)]
    ps_node = [ctx.enter_context(nc.psum_tensor(f"ps_node{k}", [W, 512], FP32)) for k in range(3)]
    LAG_SEND = 12
    with nc.Block() as block:
        @block.scalar
        def _(act):
            def mask(i, c):
                wait(act, used, fix(i, c, RING) - M + 1)
                keep = t["other_edge"][:, bass.ds(fix(i, c, RING), 1)]
                act.activation(before[:, c % M, :], t["before"][:, :], ACT.Copy, scale=keep).then_inc(masks, 1)
                act.activation(after[:, c % M, :], t["after"][:, :], ACT.Copy, scale=keep).then_inc(masks, 1)

            def carry_on(i, c):
                wait(act, sent[c % RING], (i + c // RING) * 32)
                act.activation(carry[:, c % RING, :, :].rearrange("p k v -> p (k v)"),
                               t["carry"][:, bass.ds(fix(i, c, RING), 1), :, :].rearrange("p o k v -> p (o k v)"),
                               ACT.Copy).then_inc(carried, 1)
            steps(act, [(0, mask), (10, carry_on)], 0, NT, RING)

        @block.vector
        def _(dve):
            dve.memset(zeros[:, :], 0.0).then_inc(base_in, 1)

            def one_hot(i, c):
                r, tile = c % M, fix(i, c, RING)
                wait(dve, used, tile - M + 1)
                for k in range(2):
                    dve.tensor_scalar(hotw[:, r, k, :], t["iota_win"][:, 0:NE], t["win"][:, k, bass.ds(tile, 1)], None,
                                      ALU.is_equal).then_inc(hot, 1)
                for k in range(2):
                    dve.tensor_scalar(hotp[:, r, 1 + k, :], t["iota_wh"][:, :], t["place"][:, k, bass.ds(tile, 1)], None,
                                      ALU.is_equal).then_inc(lohot, 1)
                dve.tensor_scalar(hotp[:, r, 0, :], t["iota_wh"][:, :], t["place"][:, 0, bass.ds(tile, 1)],
                                  t["self_edge"][:, bass.ds(tile, 1)], ALU.is_equal, ALU.mult).then_inc(lohot, 1)

            def read_rank(i, c):
                tile = fix(i, c, RING)
                for k in range(2):
                    dve.wait_ge(rank, tile * 2 + k + 1)
                    wait(dve, place, (i + c // RING) * 2 + (c % RING) // 8 - 1)
                    wait(dve, taken, tile * 2 + k - 1)
                    dve.tensor_tensor_reduce(junk[:, k, :], hotw[:, c % M, k, 0:NW], ps_rank[k][:, 0:NW], 1.0, 0.0, ALU.mult,
                                             ALU.add, pos[:, c % RING, k:k + 1]).then_inc(taken, 1)

            def address(i, c):
                if c % 8 != 7:
                    return
                b = i * 2 + c // 8
                half = (c % RING) // 8
                src = pos[:, half * 8:half * 8 + 8, :]
                n = [0]

                def link(ins):
                    n[0] += 1
                    ins.then_inc(place_chain, 1)
                    dve.wait_ge(place_chain, b * 6 + n[0])
                dve.wait_ge(taken, fix(i, c, RING) * 2 + 2)
                link(dve.tensor_scalar(quo[:, :, :], src, P / 2.0 - 0.5, 1.0 / P, ALU.subtract, ALU.mult))
                link(dve.tensor_scalar(quo[:, :, :], quo[:, :, :], ROUND, None, ALU.add))
                link(dve.tensor_scalar(quo[:, :, :], quo[:, :, :], ROUND, None, ALU.subtract))
                link(dve.scalar_tensor_tensor(rem[:, :, :], quo[:, :, :], -float(P), src, ALU.mult, ALU.add))
                link(dve.scalar_tensor_tensor(rem[:, :, :], rem[:, :, :], float(NS), quo[:, :, :], ALU.mult, ALU.add))
                to_self = t["self_edge"][:, bass.ds(fix(i, c, RING) - 7, 8)].unsqueeze(2).to_broadcast([P, 8, 2])
                link(dve.scalar_tensor_tensor(quo[:, :, :], to_self, 4194304.0, rem[:, :, :], ALU.mult, ALU.add))
                for j in range(8):
                    wait(dve, sent[half * 8 + j], (i + c // RING) * 32)
                dve.tensor_copy(idx[:, half * 8:half * 8 + 8, :], quo[:, :, :]).then_inc(place, 1)
            steps(dve, [(2, read_rank), (3, address), (0, one_hot)], 0, NT, RING)
            dve.wait_ge(counted, 1)
            for n, name in enumerate(("n_self", "n_in", "n_out")):
                dve.tensor_copy(t[name][:, :], ps_node[n][:, 0:NW]).then_inc(counts_sb, 1)
            ch = Chain(dve, sent_done)
            dve.wait_ge(counts_sb, 3)
            ch(dve.tensor_scalar(t["inv_in"][:, :], t["n_in"][:, :], 1.0, None, ALU.max))
            ch(dve.reciprocal(t["inv_in"][:, :], t["inv_in"][:, :]))
            ch(dve.tensor_scalar(t["inv_out"][:, :], t["n_out"][:, :], 1.0, None, ALU.max))
            ch(dve.reciprocal(t["inv_out"][:, :], t["inv_out"][:, :]))
            ch(dve.tensor_scalar(t["n_self1"][:, :], t["n_self"][:, :], 1.0, None, ALU.add))
            ch(dve.memset(t["pow"][:, :], -0.5))
            dve.wait_ge(ids, 1)
            ch(dve.tensor_scalar(t["rs_out"][:, :], t["rs_out"][:, :], float(z.n), None, ALU.is_ge))
            ch(dve.tensor_tensor(t["rs_out"][:, :], t["rs_out"][:, :], t["n_out"][:, :], ALU.add))

        @block.tensor
        def _(pe):
            pe.wait_ge(base_in, 1)
            for k in range(2):
                pe.matmul(ps_rank[k][:, 0:NW], t["ones_row"][:, :], t["base"][0:1, k, 0:NW], start=True, stop=True)
            for n in range(3):
                pe.matmul(ps_node[n][:, 0:NW], zeros[:, 0:W], zeros[:, 0:NW], start=True, stop=False)

            def ranks(i, c):
                tile, r = fix(i, c, RING), c % M
                pe.wait_ge(masks, tile * 2 + 2)
                for k in range(2):
                    pe.wait_ge(hot, tile * 2 + k + 1)
                    pe.matmul(ps_rank[k][:, 0:NW], before[:, r, :], hotw[:, r, k, 0:NW], start=False, stop=True,
                              skip_group_check=True).then_inc(rank, 1)

            def totals(i, c):
                tile, r = fix(i, c, RING), c % M
                pe.wait_ge(lohot, tile * 3 + 3)
                for n in range(3):
                    pe.matmul(ps_node[n][:, 0:NW], hotp[:, r, n, :], hotw[:, r, n // 2, 0:NW], start=False, stop=False)
                for k in range(2):
                    pe.wait_ge(taken, tile * 2 + k + 1)
                    ins = pe.matmul(ps_rank[k][:, 0:NW], after[:, r, :], hotw[:, r, k, 0:NW], start=False, stop=True,
                                    skip_group_check=True)
                ins.then_inc(used, 1)
            steps(pe, [(2, totals), (1, ranks)], 0, NT, RING)
            for n in range(3):
                ins = pe.matmul(ps_node[n][:, 0:NW], zeros[:, 0:W], zeros[:, 0:NW], start=False, stop=True)
            ins.then_inc(counted, 1)

        @block.gpsimd
        def _(pool):
            pool.iota(t["rs_out"][:, :], [[W, NW]], base=0, channel_multiplier=1, allow_small_or_imprecise_dtypes=True).then_inc(ids, 1)

            def send(i, c):
                tile, r = fix(i, c, RING), c % RING
                if c % 8 == 0:
                    wait_then_step(pool, place, i * 2 + c // 8 + 1, step)
                wait_then_step(pool, carried, tile + 1, step)
                for k in range(2):
                    pool.indirect_dma_start(dram["slots"][k], bass.IndirectOffsetOnAxis(ap=idx[:, r, k:k + 1], axis=0),
                                            carry[:, r, k, :], None, bounds_check=P * NS - 1, oob_is_err=False).then_inc(sent[r], 16)
            steps(pool, [(LAG_SEND, send)], 0, NT, RING)
            for r in range(RING):
                pool.wait_ge(sent[r], 32 * (NT // RING))
            pool.wait_ge(sent_done, 8)
            pool.tensor_tensor(t["rs_out"][:, :], t["rs_out"][:, :], t["pow"][:, 0:NW], ALU.pow).then_inc(ids, 1)
    ctx.close()
    sems.close()


def load_slots(nc, z, t, dram):
    sems = Sems(nc, "slots")
    slots_in, places = sems("slots_in"), sems("places")
    with nc.Block() as block:
        @block.sync
        def _(sp):
            for k in range(2):
                sp.dma_start(t["slot_tab"][:, k, :, :], dram["slots"][k].rearrange("(p c) v -> p c v", p=P)).then_inc(slots_in, 16)

        @block.vector
        def _(dve):
            dve.wait_ge(slots_in, 32)
            for k in range(2):
                dve.tensor_copy(t["slot_place"][:, k, :], t["slot_tab"][:, k, :, 1]).then_inc(places, 1)
    sems.close()


def slot_pass(nc, z, t, tag, kind, order, table, sums, window=None, w2=None, b2=None):
    sems = Sems(nc, tag)
    idx_ready, hot, summed, added, step, first = (sems(n) for n in ("idx_ready", "hot", "summed", "added", "step", "first"))
    got, wrote = sems("got", RING), sems("wrote", AR)
    ctx = ExitStack()
    sb = lambda name, shape, dt: ctx.enter_context(nc.sbuf_tensor(f"{tag}_{name}", shape, dt))
    R = table.shape[1]
    RO = sums.shape[-1]
    plain = kind in ("rows", "largest")
    idx = sb("idx", [P, RING], I32)
    rows = sb("rows", [P, RING, R], FP32)
    hotp = sb("hotp", [P, RING, W], BF16 if kind == "largest" else FP32)
    acc = sb("acc", [W, AR, RO], FP32)
    PS = 4 if kind == "largest" else 2
    ps_sum = [ctx.enter_context(nc.psum_tensor(f"{tag}_ps_sum{k}", [W, 512], FP32)) for k in range(PS)]
    GATHER, HOT, TURN, SPREAD, SCORE = 4, 4, 6, 9, 10
    WEIGH, SUM = {"scored": (13, 14), "attended": (15, 16)}.get(kind, (None, 8))
    ADD = SUM + 1
    if not plain:
        RW = window.shape[1]
        turned, turned_sb, spread, scored, weight, weighed = (sems(n) for n in ("turned", "turned_sb", "spread", "scored", "weight", "weighed"))
        win_in = sems("win_in", RING)
        win = sb("win", [W, RING, RW], FP32)
        hot_t = sb("hot_t", [W, 8, P], FP32)
        ps_turn = [ctx.enter_context(nc.psum_tensor(f"{tag}_ps_turn{k}", [W, 512], FP32)) for k in range(4)]
        ps_spread = [ctx.enter_context(nc.psum_tensor(f"{tag}_ps_spread{k}", [P, 512], FP32)) for k in range(2)]
    if kind == "scored":
        junk = sb("junk", [P, 2, D], FP32)
        z_e = sb("z", [P, 8], FP32)
        score = sb("score", [P, 8], FP32)
        hotw = sb("hotw", [P, 4, W], FP32)
    if kind == "attended":
        peak = sb("peak", [P, 2, SH, HEADS], FP32)
        peaked = sems("peaked")
        logit = sb("logit", [P, 2, SH, HEADS], FP32)
        slope = sb("slope", [P, SH, HEADS], FP32)
        msg = sb("msg", [P, RING, RO], FP32)
        att_chain, shifted = sems("att_chain"), sems("shifted")
    if kind == "largest":
        ident4 = sb("ident4", [P, HEADS, P], BF16)
        big = sb("big", [W, 4, HEADS], FP32)
        biggest = sems("biggest")
    sums_v = sums.rearrange("(w p) r -> w p r", p=W) if kind != "largest" else None

    with nc.Block() as block:
        def spans(run, eng):
            run(0, z.na)
            if z.na < z.ns:
                total = eng.value_load(t["total"][0:1, 0:1], min_val=0, max_val=z.ns)
                with eng.If(total > z.na):
                    run(z.na, z.ns)

        held = {}

        def window_of(eng, which, limit, slot, c):
            if c % QUAD == 0:
                a = ROUTE[which][order]
                held[which] = nc.values_load_multi_w_load_instructions(
                    t["route"][a:a + 1, bass.ds(slot, QUAD)], engines=[eng.engine], min_val=0, max_val=limit)[1]
            return held[which][c % QUAD]

        def write(eng, i, c):
            slot = fix(i, c, RING)
            w = window_of(eng, "to_win", z.nw + RING, slot, c)
            if kind == "largest":
                dst = sums[:, bass.ds(w, 1), :].rearrange("p o r -> p (o r)")
            else:
                dst = sums_v[bass.ds(w, 1), :, :].rearrange("o p r -> (o p) r")
            eng.wait_ge(added, slot + 1)
            eng.dma_start(dst, acc[:, c % AR, :]).then_inc(wrote[c % AR], 16)
        WRITE = -(-ADD // QUAD) * QUAD

        def written(eng, hi):
            for k in range(AR):
                eng.wait_ge(wrote[k], 16 * (hi // AR))

        @block.scalar
        def _(act):
            def indices(i, c):
                if c % 8 == 0:
                    wait(act, summed if plain else spread, fix(i, c, RING) - 8)
                    act.activation(idx[:, c % RING:c % RING + 8],
                                   t["slot_tab"][:, order, bass.ds(fix(i, c, RING), 8), 0], ACT.Copy).then_inc(idx_ready, 1)

            def turn_copy(i, c):
                slot = fix(i, c, RING)
                act.wait_ge(turned, slot + 1)
                wait(act, spread, slot - 7)
                act.activation(hot_t[:, c % 8, :], ps_turn[c % 4][:, 0:P], ACT.Copy).then_inc(turned_sb, 1)

            def sigmoid(i, c):
                slot = fix(i, c, RING)
                act.wait_ge(scored, slot + 1)
                wait(act, weighed, slot - 7)
                act.activation(score[:, c % 8:c % 8 + 1], z_e[:, c % 8:c % 8 + 1], ACT.Sigmoid, bias=b2).then_inc(weight, 1)

            def exponents(i, c):
                if c % SH != SH - 1:
                    return
                batch = i * (RING // SH) + c // SH
                act.wait_ge(shifted, batch + 1)
                wait(act, summed, fix(i, c, RING) - RING + 1)
                a = c % RING - SH + 1
                act.activation(msg[:, a:a + SH, HF:HF + HEADS], logit[:, (c // SH) % 2, :, :], ACT.Exp).then_inc(weight, 1)
            stages = [(0, indices)]
            if kind == "scored":
                stages = [(SCORE, sigmoid)] + stages
            if kind == "attended":
                stages = [(SCORE, exponents), (TURN, turn_copy)] + stages
            if not plain:
                stages = [(WRITE, lambda i, c: write(act, i, c))] + stages

            def run(lo, hi):
                steps(act, stages, lo, hi, RING)
                if not plain:
                    written(act, hi)
            spans(run, act)

        @block.gpsimd
        def _(pool):
            def gather(i, c):
                slot = fix(i, c, RING)
                if c % 8 == 0:
                    wait_then_step(pool, idx_ready, i * 2 + c // 8 + 1, step)
                wait_then_step(pool, summed, slot - RING + 1, step)
                pool.indirect_dma_start(rows[:, c % RING, :], None, table,
                                        bass.IndirectOffsetOnAxis(ap=idx[:, c % RING:c % RING + 1], axis=0)).then_inc(got[c % RING], 16)
            spans(lambda lo, hi: steps(pool, [(GATHER, gather)], lo, hi, RING), pool)

        @block.sync
        def _(sp):
            def load_window(i, c):
                slot = fix(i, c, RING)
                w = window_of(sp, "of_win", z.nw - 1, slot, c)
                src = window.rearrange("(w p) r -> w p r", p=W)[bass.ds(w, 1), :, :].rearrange("o p r -> (o p) r")
                if not isinstance(i, int) or slot >= RING:
                    sp.wait_ge(spread, slot - RING + 1)
                sp.dma_start(win[:, c % RING, :], src).then_inc(win_in[c % RING], 16)

            def run(lo, hi):
                steps(sp, [(WRITE, lambda i, c: write(sp, i, c))] if plain else [(0, load_window)], lo, hi, RING)
                if plain:
                    written(sp, hi)
            spans(run, sp)

        @block.vector
        def _(dve):
            if kind == "largest":
                dve.tensor_scalar(ident4[:, :, :], t["ident"][:, :].unsqueeze(1).to_broadcast([P, HEADS, P]), -BIG, None,
                                  ALU.mult).then_inc(first, 1)
            dve.memset(acc[:, :, :], 0.0).then_inc(first, 1)
            dve.wait_ge(first, 2 if kind == "largest" else 1)

            def one_hot(i, c):
                if c % QUAD:
                    return
                slot = fix(i, c, RING)
                if kind == "scored":
                    wait(dve, weighed, slot - RING + QUAD)
                    wait(dve, turned, slot - RING + QUAD)
                else:
                    wait(dve, summed, slot - RING + QUAD)
                shape = [P, QUAD, W]
                part = hotp[:, c % RING:c % RING + QUAD, :]
                place = t["slot_place"][:, order, bass.ds(slot, QUAD)].unsqueeze(2).to_broadcast(shape)
                iota = t["iota_w"][:, :].unsqueeze(1).to_broadcast(shape)
                dve.tensor_tensor(part, place, iota, ALU.not_equal if kind == "largest" else ALU.is_equal).then_inc(hot, 1)

            def turn_copy(i, c):
                slot = fix(i, c, RING)
                dve.wait_ge(turned, slot + 1)
                wait(dve, spread, slot - 7)
                dve.tensor_copy(hot_t[:, c % 8, :], ps_turn[c % 4][:, 0:P]).then_inc(turned_sb, 1)

            def add(i, c):
                slot = fix(i, c, RING)
                dve.wait_ge(summed, slot + 1)
                wait(dve, added, slot)
                wait(dve, wrote[c % AR], (i * (RING // AR) + c // AR) * 16)
                keep = t["keep"][0:W, order, bass.ds(slot, 1)]
                dve.scalar_tensor_tensor(acc[:, c % AR, :], acc[:, (c - 1) % AR, :], keep, ps_sum[c % PS][:, 0:RO], ALU.mult,
                                         ALU.add).then_inc(added, 1)

            def largest(i, c):
                slot = fix(i, c, RING)
                dve.wait_ge(summed, slot + 1)
                dve.tensor_reduce(big[:, c % 4, :], ps_sum[c % PS][:, :].rearrange("p (h f) -> p h f", h=HEADS), AX.X,
                                  ALU.max).then_inc(biggest, 1)
                wait(dve, added, slot)
                dve.wait_ge(biggest, slot + 1)
                wait(dve, wrote[c % AR], (i * (RING // AR) + c // AR) * 16)
                sink = t["sink"][0:W, bass.ds(slot, 1)]
                dve.scalar_tensor_tensor(acc[:, c % AR, :], acc[:, (c - 1) % AR, :], sink, big[:, c % 4, :], ALU.add,
                                         ALU.max).then_inc(added, 1)

            def score_edges(i, c):
                slot = fix(i, c, RING)
                dve.wait_ge(spread, slot + 1)
                wait(dve, weight, slot - 7)
                wait(dve, scored, slot - 1)
                dve.scalar_tensor_tensor(junk[:, c % 2, :], ps_spread[c % 2][:, 0:D], 0.0, w2, ALU.max, ALU.mult,
                                         accum_out=z_e[:, c % 8:c % 8 + 1]).then_inc(scored, 1)

            def weigh(i, c):
                slot = fix(i, c, RING)
                dve.wait_ge(weight, slot + 1)
                wait(dve, summed, slot - 3)
                dve.tensor_scalar(hotw[:, c % 4, :], hotp[:, c % RING, :], score[:, c % 8:c % 8 + 1], None,
                                  ALU.mult).then_inc(weighed, 1)

            def logits(i, c):
                slot = fix(i, c, RING)
                dve.wait_ge(spread, slot + 1)
                b = (c // SH) % 2
                batch = i * (RING // SH) + c // SH
                if c % SH == 0:
                    wait(dve, weight, batch - 1)
                dve.tensor_tensor(logit[:, b, c % SH, :], ps_spread[c % 2][:, 0:HEADS], rows[:, c % RING, HF:HF + HEADS],
                                  ALU.add).then_inc(scored, 1)
                dve.tensor_copy(peak[:, b, c % SH, :], ps_spread[c % 2][:, HEADS:2 * HEADS]).then_inc(peaked, 1)
                if c % SH == SH - 1:
                    dve.wait_ge(scored, slot + 1)
                    dve.wait_ge(peaked, slot + 1)
                    dve.tensor_scalar(slope[:, :, :], logit[:, b, :, :], SLOPE, None, ALU.mult).then_inc(att_chain, 1)
                    dve.wait_ge(att_chain, batch * 2 + 1)
                    dve.tensor_tensor(slope[:, :, :], slope[:, :, :], logit[:, b, :, :], ALU.max).then_inc(att_chain, 1)
                    dve.wait_ge(att_chain, batch * 2 + 2)
                    dve.tensor_tensor(logit[:, b, :, :], slope[:, :, :], peak[:, b, :, :], ALU.subtract).then_inc(shifted, 1)

            def weigh_heads(i, c):
                slot = fix(i, c, RING)
                if c % SH == 0:
                    dve.wait_ge(weight, i * (RING // SH) + c // SH + 1)
                wait(dve, summed, slot - RING + 1)
                r = c % RING
                heads = "p (h f) -> p h f"
                dve.tensor_tensor(msg[:, r, 0:HF].rearrange(heads, h=HEADS), rows[:, r, 0:HF].rearrange(heads, h=HEADS),
                                  msg[:, r, HF:HF + HEADS].unsqueeze(2).to_broadcast([P, HEADS, HID]), ALU.mult).then_inc(weighed, 1)
            stages = {"rows": [(ADD, add)], "largest": [(ADD, largest)],
                      "scored": [(ADD, add), (WEIGH, weigh), (SCORE, score_edges), (TURN + 1, turn_copy)],
                      "attended": [(ADD, add), (WEIGH, weigh_heads), (SCORE, logits)]}[kind] + [(HOT, one_hot)]
            spans(lambda lo, hi: steps(dve, stages, lo, hi, RING), dve)

        @block.tensor
        def _(pe):
            if kind == "largest":
                pe.wait_ge(first, 2)

            def got_rows(i, c):
                pe.wait_ge(got[c % RING], (i + c // RING + 1) * 16)

            def add_up(i, c):
                slot, r = fix(i, c, RING), c % RING
                if plain:
                    pe.wait_ge(hot, i * (RING // QUAD) + c // QUAD + 1)
                    got_rows(i, c)
                else:
                    pe.wait_ge(weighed, slot + 1)
                wait(pe, added, slot - PS + 1)
                if kind == "largest":
                    pe.matmul(ps_sum[c % PS][:, :], hotp[:, r, :], ident4[:, :, :].rearrange("p h f -> p (h f)"), start=True, stop=False)
                    for h in range(HEADS):
                        ins = pe.matmul(ps_sum[c % PS][:, h * P:(h + 1) * P], rows[:, r, h:h + 1].to_broadcast([P, W]),
                                        t["ident"][:, :], start=False, stop=(h == HEADS - 1))
                    ins.then_inc(summed, 1)
                    return
                lhs = hotw[:, c % 4, :] if kind == "scored" else hotp[:, r, :]
                rhs = msg[:, r, :] if kind == "attended" else rows[:, r, 0:RO]
                pe.matmul(ps_sum[c % PS][:, 0:RO], lhs, rhs, start=True, stop=True).then_inc(summed, 1)

            def turn(i, c):
                slot = fix(i, c, RING)
                pe.wait_ge(hot, i * (RING // QUAD) + c // QUAD + 1)
                wait(pe, turned_sb, slot - 3)
                pe.transpose(ps_turn[c % 4][:, 0:P], hotp[:, c % RING, :], t["ident"][:, :]).then_inc(turned, 1)

            def spread_window(i, c):
                slot, r = fix(i, c, RING), c % RING
                pe.wait_ge(turned_sb, slot + 1)
                pe.wait_ge(win_in[r], (i + c // RING + 1) * 16)
                wait(pe, scored, slot - 1)
                if kind == "attended":
                    wait(pe, peaked, slot - 1)
                got_rows(i, c)
                ins = pe.matmul(ps_spread[c % 2][:, 0:RW], hot_t[:, c % 8, :], win[:, r, :], start=True, stop=(kind == "attended"))
                if kind == "scored":
                    ins = pe.matmul(ps_spread[c % 2][:, 0:RW], t["ident"][:, :], rows[:, r, RO:RO + D], start=False, stop=True)
                ins.then_inc(spread, 1)
            stages = [(SUM, add_up)] + ([] if plain else [(SPREAD, spread_window), (TURN, turn)])
            spans(lambda lo, hi: steps(pe, stages, lo, hi, RING), pe)
    ctx.close()
    sems.close()


def group_rows(table):
    return table.rearrange("(g w p) r -> g p w r", w=G, p=W)


def group(i, c):
    return i * NRING + c


def uses(i, c, ring):
    return i * (NRING // ring) + c // ring


def load_group(eng, tile, table, loaded, i, c):
    r = c % len(loaded)
    eng.dma_start(tile[:, r, :, :], group_rows(table)[group(i, c)]).then_inc(loaded[r], 16)


def partial_group(z):
    left = z.n - (z.ng - 1) * G * W
    return left // W, left % W


def extra_dmas(z):
    full, rest = partial_group(z)
    return (full > 0) + (rest > 0) - 1


def x_group(eng, z, x, tile, sem, i, c, store=False):
    g, r = group(i, c), c % len(sem)
    if isinstance(g, int) and g == z.ng - 1:
        full, rest = partial_group(z)
        start = g * G * W
        parts = []
        if full:
            parts.append((tile[:, r, 0:full, :], x[start:start + full * W, :].rearrange("(w p) r -> p w r", p=W)))
        if rest:
            parts.append((tile[0:rest, r, full, :], x[start + full * W:z.n, :]))
    else:
        parts = [(tile[:, r, :, :], group_rows(x[0:(z.ng - 1) * G * W, :])[g])]
    for in_sb, in_dram in parts:
        to, of = (in_dram, in_sb) if store else (in_sb, in_dram)
        eng.dma_start(to, of).then_inc(sem[r], 16)


def loaded_count(z, i, c, ring, cut=False):
    g = group(i, c)
    extra = 16 * extra_dmas(z) if cut and isinstance(g, int) and g == z.ng - 1 else 0
    return (uses(i, c, ring) + 1) * 16 + extra


def wait_stores(eng, z, out, count, cut=False):
    ring = len(out)
    for r in range(ring):
        extra = 16 * extra_dmas(z) if cut and (z.ng - 1) % ring == r else 0
        wait(eng, out[r], count * len(range(r, z.ng, ring)) + extra)


class Norm:

    def __init__(self, t, sb, sems):
        self.t = t
        self.stats = sb("stats", [W, 4, G, 6], FP32)
        self.mean_var = sb("mean_var", [W, 4, G, 2], FP32)
        self.rstd = sb("rstd", [W, 4, G], FP32)
        self.stat_chain, self.var_ready, self.rstd_ready, self.normed, self.step, self.step_pool, self.centred = (
            sems(n) for n in ("stat_chain", "var_ready", "rstd_ready", "normed", "norm_step", "norm_step_pool", "centred"))

    def statistics(self, dve, i, c, r):
        g, b = group(i, c), c % 4
        wait(dve, self.normed, (g - 4 + 1) * G)
        for w in range(G):
            dve.bn_stats(self.stats[:, b, w, :], r[:, w, :]).then_inc(self.stat_chain, 1)
        wait_then_step(dve, self.stat_chain, g * 2 * G + G, self.step)
        for w in range(G):
            dve.bn_aggr(self.mean_var[:, b, w, :], self.stats[:, b, w, :]).then_inc(self.stat_chain, 1)
        dve.wait_ge(self.stat_chain, g * 2 * G + 2 * G)
        dve.tensor_scalar(self.rstd[:, b, :], self.mean_var[:, b, :, 1], EPS, None, ALU.add).then_inc(self.var_ready, 1)

    def power(self, pool, i, c):
        b = c % 4
        wait_then_step(pool, self.var_ready, group(i, c) + 1, self.step_pool)
        pool.tensor_tensor(self.rstd[:, b, :], self.rstd[:, b, :], self.t["pow"][0:W, 0:G], ALU.pow).then_inc(self.rstd_ready, 1)

    def apply(self, dve, i, c, r, out):
        g, b = group(i, c), c % 4
        dve.wait_ge(self.rstd_ready, g + 1)
        for w in range(G):
            dve.tensor_scalar(out[:, w, :], r[:, w, :], self.mean_var[:, b, w, 0:1], self.rstd[:, b, w:w + 1],
                              ALU.subtract, ALU.mult).then_inc(self.normed, 1)

    def apply_on_pool(self, pool, i, c, r, out):
        g, b = group(i, c), c % 4
        each = lambda ap: ap.unsqueeze(2).to_broadcast([W, G, D])
        wait_then_step(pool, self.rstd_ready, g + 1, self.step_pool)
        pool.tensor_tensor(r, r, each(self.mean_var[:, b, :, 0]), ALU.subtract).then_inc(self.centred, 1)
        wait_then_step(pool, self.centred, g + 1, self.step_pool)
        pool.tensor_tensor(out, r, each(self.rstd[:, b, :]), ALU.mult).then_inc(self.normed, G)


def wide(vector):
    return vector.unsqueeze(1).to_broadcast([W, G, vector.shape[-1]])


def dense0(nc, z, t, wts, dram, x):
    sems = Sems(nc, "dense0")
    ctx = ExitStack()
    sb = lambda name, shape, dt=FP32: ctx.enter_context(nc.sbuf_tensor(f"d0_{name}", shape, dt))
    ps = lambda name, shape: ctx.enter_context(nc.psum_tensor(f"d0_{name}", shape, FP32))
    S1 = D + 1
    agg, xs = sb("agg", [W, 4, G, D]), sb("x", [W, 8, G, D])
    full_sum, sum_t, res = sb("full", [W, 4, G, D]), sb("sum_t", [P, 2, G, W]), sb("res", [W, 4, G, D])
    own, other = sb("own", [W, 8, G, 2 * D + 1]), sb("other", [W, 4, G, D])
    x_t, pre, junk = sb("x_t", [P, 2, G, W]), sb("pre", [W, 4, G, D]), sb("junk", [W, G, D])
    norm = Norm(t, sb, sems)
    ps_st, ps_xt = ps("st", [P, 4, P]), ps("xt", [P, 4, P])
    ps_y, ps_u, ps_v = ([ps(f"{n}{k}", [W, 4, D]) for k in range(2)] for n in "yuv")
    summed, turned, turned_sb, product, scaled, resid = (sems(n) for n in ("summed", "turned", "turned_sb", "product", "scaled", "resid"))
    x_turned, x_turned_sb, parts, own_sb, other_sb, cleared = (sems(n) for n in ("x_turned", "x_turned_sb", "parts", "own_sb", "other_sb", "cleared"))
    weighed, edge_pre, edge_z, self_score, self_weight, pool_step = (
        sems(n) for n in ("weighed", "edge_pre", "edge_z", "self_score", "self_weight", "pool_step"))
    agg_in, x_in, out = sems("agg_in", 4), sems("x_in", 8), sems("out", 8)
    with nc.Block() as block:
        @block.sync
        def _(sp):
            sp.wait_ge(cleared, 1)

            def load(i, c):
                g = group(i, c)
                wait(sp, summed, g - 4 + 1)
                load_group(sp, agg, dram["agg"][0:z.npad, :], agg_in, i, c)
                wait(sp, resid, g - 8 + 1)
                x_group(sp, z, x, xs, x_in, i, c)

            def store(i, c):
                g, r = group(i, c), c % 8
                sp.wait_ge(own_sb, g + 1)
                sp.dma_start(group_rows(dram["own"])[g], own[:, r, :, :]).then_inc(out[r], 16)
                sp.dma_start(group_rows(dram["other"][:, 0:S1])[g], own[:, r, :, 0:S1]).then_inc(out[r], 16)
                sp.wait_ge(other_sb, g + 1)
                sp.dma_start(group_rows(dram["other"][:, S1:S1 + D])[g], other[:, c % 4, :, :]).then_inc(out[r], 16)
            steps(sp, [(14, store), (0, load)], 0, z.ng, NRING, 1)
            wait_stores(sp, z, out, 48)

        @block.gpsimd
        def _(pool):
            def self_edges(i, c):
                g = group(i, c)
                wait_then_step(pool, x_in[c % 8], loaded_count(z, i, c, 8, True), pool_step)
                wait_then_step(pool, turned, g - 4 + 1, pool_step)
                times = t["n_self"][:, bass.ds(g * G, G)].unsqueeze(2).to_broadcast([W, G, D])
                pool.tensor_tensor(full_sum[:, c % 4, :, :], xs[:, c % 8, :, :], times, ALU.mult).then_inc(weighed, 1)

            def normalize(i, c):
                wait_then_step(pool, out[c % 8], (i + c // 8) * 48, pool_step)
                wait_then_step(pool, edge_pre, group(i, c) - 8 + 1, pool_step)
                norm.apply_on_pool(pool, i, c, res[:, c % 4, :, :], own[:, c % 8, :, 0:D])

            def score_inputs(i, c):
                g = group(i, c)
                wait_then_step(pool, own_sb, g + 1, pool_step)
                wait_then_step(pool, other_sb, g + 1, pool_step)
                wait_then_step(pool, edge_z, (g - 4 + 1) * G, pool_step)
                pool.tensor_tensor(pre[:, c % 4, :, :], own[:, c % 8, :, S1:S1 + D], other[:, c % 4, :, :], ALU.add).then_inc(edge_pre, 1)
            steps(pool, [(14, score_inputs), (9, normalize), (8, lambda i, c: norm.power(pool, i, c)), (2, self_edges)], 0, z.ng, NRING, 1)

        @block.vector
        def _(dve):
            dve.memset(xs[:, :, :, :], 0.0).then_inc(cleared, 1)
            dve.memset(own[:, :, :, :], 1.0).then_inc(cleared, 1)
            dve.wait_ge(cleared, 2)

            def add_edges(i, c):
                dve.wait_ge(agg_in[c % 4], loaded_count(z, i, c, 4))
                dve.wait_ge(weighed, group(i, c) + 1)
                dve.tensor_tensor(full_sum[:, c % 4, :, :], full_sum[:, c % 4, :, :], agg[:, c % 4, :, :], ALU.add).then_inc(summed, 1)

            def residual(i, c):
                g, r = group(i, c), c % 4
                dve.wait_ge(product, g + 1)
                wait(dve, norm.normed, (g - 4 + 1) * G)
                for w in range(G):
                    ins = dve.scalar_tensor_tensor(res[:, r, w, :], ps_y[c % 2][:, w, :], t["rs_out"][:, bass.ds(g * G + w, 1)],
                                                   wts["L0_bias"][0:W, :], ALU.mult, ALU.add)
                ins.then_inc(scaled, 1)
                dve.wait_ge(scaled, g + 1)
                dve.scalar_tensor_tensor(res[:, r, :, :], res[:, r, :, :], 0.0, xs[:, c % 8, :, :], ALU.max, ALU.add).then_inc(resid, 1)
                dve.wait_ge(resid, g + 1)
                norm.statistics(dve, i, c, res[:, r, :, :])

            def other_part(i, c):
                g, r = group(i, c), c % 8
                dve.wait_ge(parts, g + 1)
                wait(dve, out[(c - 4) % 8], (i + (c - 4) // 8 + 1) * 48)
                wait(dve, edge_pre, g - 4 + 1)
                dve.tensor_tensor(other[:, c % 4, :, :], ps_v[c % 2][:, 0:G, :], wide(wts["L1_b_e1"][0:W, :]), ALU.add).then_inc(other_sb, 1)

            def self_scores(i, c):
                g = group(i, c)
                dve.wait_ge(edge_pre, g + 1)
                wait(dve, edge_z, g * G)
                for w in range(G):
                    dve.scalar_tensor_tensor(junk[:, w, :], pre[:, c % 4, w, :], 0.0, wts["L1_w_e2"][0:W, :], ALU.max,
                                             ALU.mult, accum_out=t["self_w"][:, bass.ds(g * G + w, 1)]).then_inc(edge_z, 1)
            steps(dve, [(15, self_scores), (13, other_part), (7, residual), (3, add_edges)], 0, z.ng, NRING, 1)
            dve.wait_ge(self_score, 1)
            dve.tensor_tensor(t["self_w"][:, :], t["self_w"][:, :], t["n_self"][:, :], ALU.mult).then_inc(self_weight, 1)

        @block.scalar
        def _(act):
            def copy_sum(i, c):
                g = group(i, c)
                act.wait_ge(turned, g + 1)
                wait(act, product, g - 2 + 1)
                act.activation(sum_t[:, c % 2, :, :], ps_st[:, 0:G, 0:W], ACT.Copy).then_inc(turned_sb, 1)

            def copy_x(i, c):
                g = group(i, c)
                act.wait_ge(x_turned, g + 1)
                wait(act, parts, g - 2 + 1)
                act.activation(x_t[:, c % 2, :, :], ps_xt[:, 0:G, 0:W], ACT.Copy).then_inc(x_turned_sb, 1)

            def own_part(i, c):
                g = group(i, c)
                act.wait_ge(parts, g + 1)
                wait(act, out[c % 8], (i + c // 8) * 48)
                act.activation(own[:, c % 8, :, S1:S1 + D], ps_u[c % 2][:, 0:G, :], ACT.Copy).then_inc(own_sb, 1)
            steps(act, [(5, copy_sum), (12, copy_x), (13, own_part)], 0, z.ng, NRING, 1)
            act.wait_ge(edge_z, z.nw)
            act.activation(t["self_w"][:, :], t["self_w"][:, :], ACT.Sigmoid, bias=wts["L1_b_e2"][0:W, :]).then_inc(self_score, 1)

        @block.tensor
        def _(pe):
            def turn(i, c):
                g = group(i, c)
                pe.wait_ge(summed, g + 1)
                wait(pe, turned_sb, g)
                for w in range(G):
                    ins = pe.transpose(ps_st[:, w, 0:W], full_sum[:, c % 4, w, :], t["ident"][0:W, 0:W])
                ins.then_inc(turned, 1)

            def multiply(i, c):
                g = group(i, c)
                pe.wait_ge(turned_sb, g + 1)
                wait(pe, scaled, g - 2 + 1)
                for w in range(G):
                    ins = pe.matmul(ps_y[c % 2][:, w, :], sum_t[:, c % 2, w, :], wts["L0_kernel"][:, :], start=True, stop=True)
                ins.then_inc(product, 1)

            def turn_x(i, c):
                g = group(i, c)
                pe.wait_ge(norm.normed, (g + 1) * G)
                wait(pe, x_turned_sb, g)
                for w in range(G):
                    ins = pe.transpose(ps_xt[:, w, 0:W], own[:, c % 8, w, 0:D], t["ident"][0:W, 0:W])
                ins.then_inc(x_turned, 1)

            def score_parts(i, c):
                g = group(i, c)
                pe.wait_ge(x_turned_sb, g + 1)
                wait(pe, own_sb, g - 2 + 1)
                wait(pe, other_sb, g - 2 + 1)
                for w in range(G):
                    pe.matmul(ps_u[c % 2][:, w, :], x_t[:, c % 2, w, :], wts["L1_w_e1"][:, 0:D], start=True, stop=True)
                    ins = pe.matmul(ps_v[c % 2][:, w, :], x_t[:, c % 2, w, :], wts["L1_w_e1"][:, D:2 * D], start=True, stop=True)
                ins.then_inc(parts, 1)
            steps(pe, [(12, score_parts), (11, turn_x), (6, multiply), (4, turn)], 0, z.ng, NRING, 1)
    ctx.close()
    sems.close()


def dense1(nc, z, t, wts, dram):
    sems = Sems(nc, "dense1")
    ctx = ExitStack()
    sb = lambda name, shape, dt=FP32: ctx.enter_context(nc.sbuf_tensor(f"d1_{name}", shape, dt))
    ps = lambda name, shape: ctx.enter_context(nc.psum_tensor(f"d1_{name}", shape, FP32))
    S1 = D + 1
    sums = [sb("sum_in", [W, 4, G, S1]), sb("sum_out", [W, 4, G, S1])]
    own, xs, junk = sb("own", [W, 4, G, S1]), sb("x", [W, 4, G, D]), sb("junk", [W, G, D])
    mean = [sb(f"mean{k}", [W, 4, G, S1]) for k in range(2)]
    mean_t = [sb(f"mean_t{k}", [P, 2, G, W]) for k in range(2)]
    hid = [sb("hid0", [W, 4, G, D]), sb("hid1", [W, 8, G, D])]
    hid_t = [sb(f"hid_t{k}", [P, 2, G, W]) for k in range(2)]
    gate_in, z_g, gate = sb("gate_in", [W, 2, G, D]), sb("z_g", [W, 4, G]), sb("gate", [W, 4, G])
    res, rest, new = sb("res", [W, 8, G, D]), sb("rest", [W, 4, G, D]), sb("new", [W, 4, G, D])
    norm = Norm(t, sb, sems)
    ps_mt = [ps(f"mt{k}", [P, 4, P]) for k in range(2)]
    ps_h = [ps(f"h{k}", [W, 4, D]) for k in range(2)]
    ps_ht = [ps(f"ht{k}", [P, 4, P]) for k in range(2)]
    ps_g = [ps(f"g{k}", [W, 4, D]) for k in range(2)]
    own_in, x_in, sum_in, out = sems("own_in", 4), sems("x_in", 4), [sems("s_in", 4), sems("s_out", 4)], sems("out", 4)
    (summed, scaled, turned, turned_sb, product, hidden, h_turned, h_turned_sb, gated, gate_pre, gate_z, gate_on, diff,
     doubled, rested, resid, own_weighed, pool_step) = (
        sems(n) for n in ("summed", "scaled", "turned", "turned_sb", "product", "hidden", "h_turned", "h_turned_sb", "gated", "gate_pre",
                          "gate_z", "gate_on", "diff", "doubled", "rested", "resid", "own_weighed", "pool_step"))
    inv = (t["inv_in"], t["inv_out"])
    bias = (wts["L1_b_s2d"], wts["L1_b_d2s"])
    w_dir = (wts["L1_w_s2d"], wts["L1_w_d2s"])
    with nc.Block() as block:
        @block.sync
        def _(sp):
            def load(i, c):
                g = group(i, c)
                wait(sp, summed, g - 4 + 1)
                load_group(sp, own, dram["own"][:, 0:S1], own_in, i, c)
                wait(sp, scaled, (g - 4 + 1) * 2 * G)
                for k, name in enumerate(("sum_in", "sum_out")):
                    load_group(sp, sums[k], dram[name][0:z.npad, :], sum_in[k], i, c)

            def load_x(i, c):
                wait(sp, rested, group(i, c) - 4 + 1)
                load_group(sp, xs, dram["own"][:, 0:D], x_in, i, c)

            def store(i, c):
                sp.wait_ge(norm.normed, (group(i, c) + 1) * G)
                sp.dma_start(group_rows(dram["x2"])[group(i, c)], new[:, c % 4, :, :]).then_inc(out[c % 4], 16)
            steps(sp, [(17, store), (9, load_x), (0, load)], 0, z.ng, NRING, 1)
            wait_stores(sp, z, out, 16)

        @block.gpsimd
        def _(pool):
            def weigh_own(i, c):
                g, r = group(i, c), c % 4
                wait_then_step(pool, own_in[r], loaded_count(z, i, c, 4), pool_step)
                score = t["self_w"][:, bass.ds(g * G, G)].unsqueeze(2).to_broadcast([W, G, S1])
                pool.tensor_tensor(own[:, r, :, :], own[:, r, :, :], score, ALU.mult).then_inc(own_weighed, 1)

            def difference(i, c):
                g = group(i, c)
                wait_then_step(pool, hidden, g + 1, pool_step)
                wait_then_step(pool, norm.normed, (g - 8 + 1) * G, pool_step)
                pool.tensor_tensor(res[:, c % 8, :, :], hid[0][:, c % 4, :, :], hid[1][:, c % 8, :, :], ALU.subtract).then_inc(diff, 1)

            def rest_of_sum(i, c):
                g, r = group(i, c), c % 4
                wait_then_step(pool, doubled, g + 1, pool_step)
                wait_then_step(pool, resid, g - 4 + 1, pool_step)
                pool.tensor_tensor(rest[:, r, :, :], xs[:, r, :, :], hid[1][:, c % 8, :, :], ALU.add).then_inc(rested, 1)

            def normalize(i, c):
                wait_then_step(pool, out[c % 4], uses(i, c, 4) * 16, pool_step)
                norm.apply_on_pool(pool, i, c, res[:, c % 8, :, :], new[:, c % 4, :, :])
            steps(pool, [(16, normalize), (15, lambda i, c: norm.power(pool, i, c)), (13, rest_of_sum), (9, difference), (2, weigh_own)],
                  0, z.ng, NRING, 1)

        @block.vector
        def _(dve):
            def add_self(i, c):
                g, r = group(i, c), c % 4
                dve.wait_ge(own_weighed, g + 1)
                for k in range(2):
                    dve.wait_ge(sum_in[k][r], loaded_count(z, i, c, 4))
                    ins = dve.tensor_tensor(sums[k][:, r, :, :], sums[k][:, r, :, :], own[:, r, :, :], ALU.add)
                ins.then_inc(summed, 1)

            def hiddens(i, c):
                g = group(i, c)
                dve.wait_ge(product, g + 1)
                wait(dve, diff, g - 4 + 1)
                wait(dve, h_turned, g - 4 + 1)
                wait(dve, rested, g - 8 + 1)
                for k in range(2):
                    for w in range(G):
                        ins = dve.scalar_tensor_tensor(hid[k][:, c % (4, 8)[k], w, :], bias[k][0:W, :], mean[k][:, c % 4, w, D:S1],
                                                       ps_h[k][:, w, :], ALU.mult, ALU.add)
                ins.then_inc(hidden, 1)

            def gates(i, c):
                g, r = group(i, c), c % 4
                dve.wait_ge(gated, g + 1)
                dve.tensor_tensor(gate_in[:, c % 2, :, :], ps_g[c % 2][:, 0:G, :], wide(wts["L1_b_g1"][0:W, :]), ALU.add).then_inc(gate_pre, 1)
                dve.wait_ge(gate_pre, g + 1)
                wait(dve, gate_on, g - 4 + 1)
                wait(dve, gate_z, g)
                for w in range(G):
                    ins = dve.scalar_tensor_tensor(junk[:, w, :], gate_in[:, c % 2, w, :], 0.0, wts["L1_w_g2"][0:W, :], ALU.max,
                                                   ALU.mult, accum_out=z_g[:, r, w:w + 1])
                ins.then_inc(gate_z, 1)

            def mix(i, c):
                g, r = group(i, c), c % 4
                dve.wait_ge(gate_on, g + 1)
                dve.wait_ge(rested, g + 1)
                for w in range(G):
                    ins = dve.scalar_tensor_tensor(res[:, c % 8, w, :], res[:, c % 8, w, :], gate[:, r, w:w + 1], rest[:, r, w, :],
                                                   ALU.mult, ALU.add)
                ins.then_inc(resid, 1)
                dve.wait_ge(resid, g + 1)
                norm.statistics(dve, i, c, res[:, c % 8, :, :])
            steps(dve, [(14, mix), (12, gates), (8, hiddens), (3, add_self)], 0, z.ng, NRING, 1)

        @block.scalar
        def _(act):
            def scale(i, c):
                g, r = group(i, c), c % 4
                act.wait_ge(summed, g + 1)
                wait(act, hidden, g - 4 + 1)
                for k in range(2):
                    for w in range(G):
                        act.activation(mean[k][:, r, w, :], sums[k][:, r, w, :], ACT.Copy,
                                       scale=inv[k][:, bass.ds(g * G + w, 1)]).then_inc(scaled, 1)

            def copy_means(i, c):
                g = group(i, c)
                act.wait_ge(turned, g + 1)
                wait(act, product, g - 2 + 1)
                for k in range(2):
                    ins = act.activation(mean_t[k][:, c % 2, :, :], ps_mt[k][:, 0:G, 0:W], ACT.Copy)
                ins.then_inc(turned_sb, 1)

            def copy_hiddens(i, c):
                g = group(i, c)
                act.wait_ge(h_turned, g + 1)
                wait(act, gated, g - 2 + 1)
                for k in range(2):
                    ins = act.activation(hid_t[k][:, c % 2, :, :], ps_ht[k][:, 0:G, 0:W], ACT.Copy)
                ins.then_inc(h_turned_sb, 1)

            def sigmoid_gate(i, c):
                g, r = group(i, c), c % 4
                act.wait_ge(gate_z, g + 1)
                wait(act, resid, g - 4 + 1)
                act.activation(gate[:, r, :], z_g[:, r, :], ACT.Sigmoid, bias=wts["L1_b_g2"][0:W, :]).then_inc(gate_on, 1)

            def double_x(i, c):
                act.wait_ge(x_in[c % 4], loaded_count(z, i, c, 4))
                act.activation(xs[:, c % 4, :, :], xs[:, c % 4, :, :], ACT.Copy, scale=2.0).then_inc(doubled, 1)
            steps(act, [(6, copy_means), (10, copy_hiddens), (13, sigmoid_gate), (12, double_x), (4, scale)], 0, z.ng, NRING, 1)

        @block.tensor
        def _(pe):
            def turn_means(i, c):
                g = group(i, c)
                pe.wait_ge(scaled, (g + 1) * 2 * G)
                wait(pe, turned_sb, g)
                for k in range(2):
                    for w in range(G):
                        ins = pe.transpose(ps_mt[k][:, w, 0:W], mean[k][:, c % 4, w, 0:D], t["ident"][0:W, 0:W])
                ins.then_inc(turned, 1)

            def multiply(i, c):
                g = group(i, c)
                pe.wait_ge(turned_sb, g + 1)
                wait(pe, hidden, g)
                for k in range(2):
                    for w in range(G):
                        ins = pe.matmul(ps_h[k][:, w, :], mean_t[k][:, c % 2, w, :], w_dir[k][:, :], start=True, stop=True)
                ins.then_inc(product, 1)

            def turn_hiddens(i, c):
                g = group(i, c)
                pe.wait_ge(hidden, g + 1)
                wait(pe, h_turned_sb, g)
                for k in range(2):
                    for w in range(G):
                        ins = pe.transpose(ps_ht[k][:, w, 0:W], hid[k][:, c % (4, 8)[k], w, :], t["ident"][0:W, 0:W])
                ins.then_inc(h_turned, 1)

            def gate_product(i, c):
                g = group(i, c)
                pe.wait_ge(h_turned_sb, g + 1)
                wait(pe, gate_pre, g - 2 + 1)
                for w in range(G):
                    for k in range(2):
                        ins = pe.matmul(ps_g[c % 2][:, w, :], hid_t[k][:, c % 2, w, :], wts["L1_w_g1"][:, k * D:(k + 1) * D],
                                        start=(k == 0), stop=(k == 1))
                ins.then_inc(gated, 1)
            steps(pe, [(11, gate_product), (9, turn_hiddens), (7, multiply), (5, turn_means)], 0, z.ng, NRING, 1)
    ctx.close()
    sems.close()


def dense2a(nc, z, t, wts, dram):
    sems = Sems(nc, "dense2a")
    ctx = ExitStack()
    sb = lambda name, shape, dt=FP32: ctx.enter_context(nc.sbuf_tensor(f"d2a_{name}", shape, dt))
    ps = lambda name, shape: ctx.enter_context(nc.psum_tensor(f"d2a_{name}", shape, FP32))
    agg, xs, mean = sb("agg", [W, 4, G, D]), sb("x", [W, 8, G, D]), sb("mean", [W, 2, G, D])
    mean_t, x_t, h = sb("mean_t", [P, 2, G, W]), sb("x_t", [P, 2, G, W]), sb("h", [W, 4, G, D])
    pre = sb("pre", [W, 2, G, D])
    ps_m, ps_x = ([ps(f"{n}{k}", [P, 4, P]) for k in range(2)] for n in "mx")
    ps_h = [ps(f"h{k}", [W, 4, D]) for k in range(2)]
    summed, scaled, turned, turned_sb, product, biased, relued = (sems(n) for n in (
        "summed", "scaled", "turned", "turned_sb", "product", "biased", "relued"))
    agg_in, x_in, out = sems("agg_in", 4), sems("x_in", 8), sems("out", 4)
    with nc.Block() as block:
        @block.sync
        def _(sp):
            def load(i, c):
                g = group(i, c)
                wait(sp, scaled, (g - 4 + 1) * G)
                load_group(sp, agg, dram["agg2"][0:z.npad, :], agg_in, i, c)
                wait(sp, turned, g - 8 + 1)
                load_group(sp, xs, dram["x2"], x_in, i, c)

            def store(i, c):
                sp.wait_ge(relued, group(i, c) + 1)
                sp.dma_start(group_rows(dram["h"])[group(i, c)], h[:, c % 4, :, :]).then_inc(out[c % 4], 16)
            steps(sp, [(10, store), (0, load)], 0, z.ng, NRING, 1)
            wait_stores(sp, z, out, 16)

        @block.vector
        def _(dve):
            def self_edges(i, c):
                g = group(i, c)
                dve.wait_ge(agg_in[c % 4], loaded_count(z, i, c, 4))
                dve.wait_ge(x_in[c % 8], loaded_count(z, i, c, 8))
                for w in range(G):
                    ins = dve.scalar_tensor_tensor(agg[:, c % 4, w, :], xs[:, c % 8, w, :], t["n_self"][:, bass.ds(g * G + w, 1)],
                                                   agg[:, c % 4, w, :], ALU.mult, ALU.add)
                ins.then_inc(summed, 1)

            def add_bias(i, c):
                g = group(i, c)
                dve.wait_ge(product, g + 1)
                wait(dve, relued, g - 2 + 1)
                dve.tensor_tensor(pre[:, c % 2, :, :], ps_h[c % 2][:, 0:G, :], wide(wts["L2_f_lb"][0:W, :]), ALU.add).then_inc(biased, 1)
            steps(dve, [(8, add_bias), (3, self_edges)], 0, z.ng, NRING, 1)

        @block.scalar
        def _(act):
            def scale(i, c):
                g = group(i, c)
                act.wait_ge(summed, g + 1)
                wait(act, turned, g - 2 + 1)
                for w in range(G):
                    act.activation(mean[:, c % 2, w, :], agg[:, c % 4, w, :], ACT.Copy,
                                   scale=t["inv_in"][:, bass.ds(g * G + w, 1)]).then_inc(scaled, 1)

            def copy_turned(i, c):
                g = group(i, c)
                act.wait_ge(turned, g + 1)
                wait(act, product, g - 2 + 1)
                act.activation(mean_t[:, c % 2, :, :], ps_m[c % 2][:, 0:G, 0:W], ACT.Copy)
                act.activation(x_t[:, c % 2, :, :], ps_x[c % 2][:, 0:G, 0:W], ACT.Copy).then_inc(turned_sb, 1)

            def relu(i, c):
                act.wait_ge(biased, group(i, c) + 1)
                wait(act, out[c % 4], uses(i, c, 4) * 16)
                act.activation(h[:, c % 4, :, :], pre[:, c % 2, :, :], ACT.Relu).then_inc(relued, 1)
            steps(act, [(9, relu), (6, copy_turned), (4, scale)], 0, z.ng, NRING, 1)

        @block.tensor
        def _(pe):
            def turn(i, c):
                g = group(i, c)
                pe.wait_ge(scaled, (g + 1) * G)
                pe.wait_ge(x_in[c % 8], loaded_count(z, i, c, 8))
                wait(pe, turned_sb, g - 2 + 1)
                for w in range(G):
                    pe.transpose(ps_m[c % 2][:, w, 0:W], mean[:, c % 2, w, :], t["ident"][0:W, 0:W])
                for w in range(G):
                    ins = pe.transpose(ps_x[c % 2][:, w, 0:W], xs[:, c % 8, w, :], t["ident"][0:W, 0:W])
                ins.then_inc(turned, 1)

            def multiply(i, c):
                g = group(i, c)
                pe.wait_ge(turned_sb, g + 1)
                wait(pe, biased, g - 2 + 1)
                for w in range(G):
                    pe.matmul(ps_h[c % 2][:, w, :], mean_t[:, c % 2, w, :], wts["L2_f_lwT"][:, :], start=True, stop=False)
                    ins = pe.matmul(ps_h[c % 2][:, w, :], x_t[:, c % 2, w, :], wts["L2_f_rwT"][:, :], start=False, stop=True)
                ins.then_inc(product, 1)
            steps(pe, [(7, multiply), (5, turn)], 0, z.ng, NRING, 1)
    ctx.close()
    sems.close()


def dense2b(nc, z, t, wts, dram):
    sems = Sems(nc, "dense2b")
    ctx = ExitStack()
    sb = lambda name, shape, dt=FP32: ctx.enter_context(nc.sbuf_tensor(f"d2b_{name}", shape, dt))
    ps = lambda name, shape: ctx.enter_context(nc.psum_tensor(f"d2b_{name}", shape, FP32))
    HT = HF + 2 * HEADS
    agg, hs, xs, mean = sb("agg", [W, 4, G, D]), sb("h", [W, 8, G, D]), sb("x", [W, 8, G, D]), sb("mean", [W, 2, G, D])
    parts_t = [sb(f"parts_t{k}", [P, 2, G, W]) for k in range(3)]
    res, new, new_t = sb("res", [W, 4, G, D]), sb("new", [W, 4, G, D]), sb("new_t", [P, 2, G, W])
    heads = sb("heads", [W, 4, G, HT])
    norm = Norm(t, sb, sems)
    ps_t, ps_y, ps_n, ps_w = [ps(f"t{k}", [P, 4, P]) for k in range(3)], ps("y", [W, 4, D]), ps("n", [P, 4, P]), ps("w", [W, G, 512])
    summed, scaled, turned, turned_sb, product, biased, resid, n_turned, n_turned_sb, headed, heads_sb, terms = (sems(n) for n in (
        "summed", "scaled", "turned", "turned_sb", "product", "biased", "resid", "n_turned", "n_turned_sb", "headed", "heads_sb", "terms"))
    agg_in, h_in, x_in, out, h_out, a_out = sems("agg_in", 4), sems("h_in", 8), sems("x_in", 8), sems("out", 4), sems("h_out", 4), sems("a_out")
    with nc.Block() as block:
        @block.sync
        def _(sp):
            def load(i, c):
                g = group(i, c)
                wait(sp, scaled, (g - 4 + 1) * G)
                load_group(sp, agg, dram["agg3"][0:z.npad, :], agg_in, i, c)
                wait(sp, turned, g - 8 + 1)
                load_group(sp, hs, dram["h"], h_in, i, c)
                wait(sp, resid, g - 8 + 1)
                load_group(sp, xs, dram["x2"], x_in, i, c)

            def store_x(i, c):
                sp.wait_ge(norm.normed, (group(i, c) + 1) * G)
                sp.dma_start(group_rows(dram["x3"])[group(i, c)], new[:, c % 4, :, :]).then_inc(out[c % 4], 16)

            def store_heads(i, c):
                sp.wait_ge(heads_sb, group(i, c) + 1)
                sp.dma_start(group_rows(dram["heads"])[group(i, c)], heads[:, c % 4, :, 0:HF + HEADS]).then_inc(h_out[c % 4], 16)
            steps(sp, [(15, store_heads), (12, store_x), (0, load)], 0, z.ng, NRING, 1)
            wait_stores(sp, z, out, 16)
            wait_stores(sp, z, h_out, 16)
            sp.wait_ge(terms, z.ng)
            sp.dma_start(dram["a_src"].rearrange("(w p) h -> p w h", p=W), t["a_src"][:, :, :]).then_inc(a_out, 16)
            sp.wait_ge(a_out, 16)

        @block.gpsimd
        def _(pool):
            steps(pool, [(9, lambda i, c: norm.power(pool, i, c))], 0, z.ng, NRING, 1)

        @block.vector
        def _(dve):
            def self_edges(i, c):
                g = group(i, c)
                dve.wait_ge(agg_in[c % 4], loaded_count(z, i, c, 4))
                dve.wait_ge(h_in[c % 8], loaded_count(z, i, c, 8))
                for w in range(G):
                    ins = dve.scalar_tensor_tensor(agg[:, c % 4, w, :], hs[:, c % 8, w, :], t["n_self"][:, bass.ds(g * G + w, 1)],
                                                   agg[:, c % 4, w, :], ALU.mult, ALU.add)
                ins.then_inc(summed, 1)

            def residual(i, c):
                g, r = group(i, c), c % 4
                dve.wait_ge(product, g + 1)
                wait(dve, norm.normed, (g - 4 + 1) * G)
                dve.tensor_tensor(res[:, r, :, :], ps_y[:, 0:G, :], wide(wts["L2_bias"][0:W, :]), ALU.add).then_inc(biased, 1)
                dve.wait_ge(biased, g + 1)
                dve.wait_ge(x_in[c % 8], loaded_count(z, i, c, 8))
                dve.scalar_tensor_tensor(res[:, r, :, :], res[:, r, :, :], 0.0, xs[:, c % 8, :, :], ALU.max, ALU.add).then_inc(resid, 1)
                dve.wait_ge(resid, g + 1)
                norm.statistics(dve, i, c, res[:, r, :, :])

            def normalize(i, c):
                wait(dve, out[c % 4], uses(i, c, 4) * 16)
                wait(dve, n_turned, group(i, c) - 4 + 1)
                norm.apply(dve, i, c, res[:, c % 4, :, :], new[:, c % 4, :, :])

            def attention_terms(i, c):
                g = group(i, c)
                dve.wait_ge(heads_sb, g + 1)
                dve.tensor_copy(t["a_src"][:, bass.ds(g * G, G), :], heads[:, c % 4, :, HF:HF + HEADS])
                dve.tensor_copy(t["a_dst"][:, bass.ds(g * G, G), :], heads[:, c % 4, :, HF + HEADS:HT]).then_inc(terms, 1)
            steps(dve, [(8, residual), (11, normalize), (16, attention_terms), (3, self_edges)], 0, z.ng, NRING, 1)

        @block.scalar
        def _(act):
            def scale(i, c):
                g = group(i, c)
                act.wait_ge(summed, g + 1)
                wait(act, turned, g - 2 + 1)
                for w in range(G):
                    act.activation(mean[:, c % 2, w, :], agg[:, c % 4, w, :], ACT.Copy,
                                   scale=t["inv_in"][:, bass.ds(g * G + w, 1)]).then_inc(scaled, 1)

            def copy_turned(i, c):
                g = group(i, c)
                act.wait_ge(turned, g + 1)
                wait(act, product, g - 2 + 1)
                for k in range(3):
                    ins = act.activation(parts_t[k][:, c % 2, :, :], ps_t[k][:, 0:G, 0:W], ACT.Copy)
                ins.then_inc(turned_sb, 1)

            def copy_new(i, c):
                g = group(i, c)
                act.wait_ge(n_turned, g + 1)
                wait(act, headed, g - 2 + 1)
                act.activation(new_t[:, c % 2, :, :], ps_n[:, 0:G, 0:W], ACT.Copy).then_inc(n_turned_sb, 1)

            def copy_heads(i, c):
                g = group(i, c)
                act.wait_ge(headed, g + 1)
                wait(act, h_out[c % 4], uses(i, c, 4) * 16)
                wait(act, terms, g - 4 + 1)
                act.activation(heads[:, c % 4, :, :], ps_w[:, :, 0:HT], ACT.Copy).then_inc(heads_sb, 1)
            steps(act, [(13, copy_new), (15, copy_heads), (6, copy_turned), (4, scale)], 0, z.ng, NRING, 1)

        @block.tensor
        def _(pe):
            def turn(i, c):
                g = group(i, c)
                pe.wait_ge(scaled, (g + 1) * G)
                pe.wait_ge(h_in[c % 8], loaded_count(z, i, c, 8))
                pe.wait_ge(x_in[c % 8], loaded_count(z, i, c, 8))
                wait(pe, turned_sb, g)
                for k, of in enumerate((mean[:, c % 2, :, :], hs[:, c % 8, :, :], xs[:, c % 8, :, :])):
                    for w in range(G):
                        ins = pe.transpose(ps_t[k][:, w, 0:W], of[:, w, :], t["ident"][0:W, 0:W])
                ins.then_inc(turned, 1)

            def multiply(i, c):
                g = group(i, c)
                pe.wait_ge(turned_sb, g + 1)
                wait(pe, biased, g)
                for w in range(G):
                    for k, name in enumerate(("L2_n_lwT", "L2_n_rwT", "L2_fc_wT")):
                        ins = pe.matmul(ps_y[:, w, :], parts_t[k][:, c % 2, w, :], wts[name][:, :], start=(k == 0), stop=(k == 2))
                ins.then_inc(product, 1)

            def turn_new(i, c):
                g = group(i, c)
                pe.wait_ge(norm.normed, (g + 1) * G)
                wait(pe, n_turned_sb, g)
                for w in range(G):
                    ins = pe.transpose(ps_n[:, w, 0:W], new[:, c % 4, w, :], t["ident"][0:W, 0:W])
                ins.then_inc(n_turned, 1)

            def head_product(i, c):
                g = group(i, c)
                pe.wait_ge(n_turned_sb, g + 1)
                wait(pe, heads_sb, g)
                for w in range(G):
                    ins = pe.matmul(ps_w[:, w, 0:HT], new_t[:, c % 2, w, :], wts["L3_W"][:, :], start=True, stop=True)
                ins.then_inc(headed, 1)
            steps(pe, [(12, turn_new), (7, multiply), (14, head_product), (5, turn)], 0, z.ng, NRING, 1)
    ctx.close()
    sems.close()


def shifts(nc, z, t, dram):
    sems = Sems(nc, "shifts")
    big_in, chain, rows_out, exps = sems("big_in"), sems("chain"), sems("rows_out"), sems("exps")
    ctx = ExitStack()
    sb = lambda name, shape, dt=FP32: ctx.enter_context(nc.sbuf_tensor(f"sh_{name}", shape, dt))
    NW = z.nw
    big, top, own, low = (sb(n, [W, NW, HEADS]) for n in ("big", "top", "own", "low"))
    rows = sb("rows", [W, NW, 2 * HEADS])
    with nc.Block() as block:
        @block.sync
        def _(sp):
            sp.dma_start(big[:, :, :], dram["largest"][:, 0:NW, :]).then_inc(big_in, 16)
            sp.wait_ge(chain, 6)
            sp.dma_start(dram["shift"].rearrange("(w p) h -> p w h", p=W), rows[:, :, :]).then_inc(rows_out, 16)
            sp.wait_ge(rows_out, 16)

        @block.scalar
        def _(act):
            act.wait_ge(chain, 10)
            act.activation(own[:, :, :], own[:, :, :], ACT.Exp).then_inc(exps, 1)

        @block.vector
        def _(dve):
            ch = Chain(dve, chain)
            dve.wait_ge(big_in, 16)
            ch(dve.tensor_tensor(top[:, :, :], big[:, :, :], t["a_src"][:, :, :], ALU.max))
            ch(dve.tensor_tensor(top[:, :, :], top[:, :, :], t["a_dst"][:, :, :], ALU.add))
            ch(dve.tensor_scalar(low[:, :, :], top[:, :, :], SLOPE, None, ALU.mult))
            ch(dve.tensor_tensor(top[:, :, :], top[:, :, :], low[:, :, :], ALU.max))
            ch(dve.tensor_copy(rows[:, :, 0:HEADS], t["a_dst"][:, :, :]))
            ch(dve.tensor_copy(rows[:, :, HEADS:2 * HEADS], top[:, :, :]))
            ch(dve.tensor_tensor(own[:, :, :], t["a_src"][:, :, :], t["a_dst"][:, :, :], ALU.add))
            ch(dve.tensor_scalar(low[:, :, :], own[:, :, :], SLOPE, None, ALU.mult))
            ch(dve.tensor_tensor(own[:, :, :], own[:, :, :], low[:, :, :], ALU.max))
            ch(dve.tensor_tensor(own[:, :, :], own[:, :, :], top[:, :, :], ALU.subtract))
            dve.wait_ge(exps, 1)
            ch(dve.tensor_tensor(t["ex_self"][:, :, :], own[:, :, :], t["n_self1"][:, :].unsqueeze(2).to_broadcast([W, NW, HEADS]), ALU.mult))
    ctx.close()
    sems.close()


def dense3(nc, z, t, wts, dram, result):
    sems = Sems(nc, "dense3")
    ctx = ExitStack()
    sb = lambda name, shape, dt=FP32: ctx.enter_context(nc.sbuf_tensor(f"d3_{name}", shape, dt))
    ps = lambda name, shape: ctx.enter_context(nc.psum_tensor(f"d3_{name}", shape, FP32))
    att, heads, xs = sb("att", [W, 4, G, HF + HEADS]), sb("heads", [W, 4, G, HF + HEADS]), sb("x", [W, 4, G, D])
    den, mixed = sb("den", [W, 2, G, HEADS]), sb("mixed", [W, 4, G, HF])
    relu_t = sb("relu_t", [P, 2, 2, G, W])
    res, new = sb("res", [W, 4, G, D]), sb("new", [W, 4, G, D])
    norm = Norm(t, sb, sems)
    ps_t, ps_y = [[ps(f"t{n}{k}", [P, 4, P]) for k in range(2)] for n in range(2)], [ps(f"y{k}", [W, 4, D]) for k in range(2)]
    owned, summed, denom, denom_inv, divided, turned, turned_sb, product, x_biased, resid, pool_step = (sems(n) for n in (
        "owned", "summed", "denom", "denom_inv", "divided", "turned", "turned_sb", "product", "x_biased", "resid", "pool_step"))
    att_in, heads_in, x_in, out = sems("att_in", 4), sems("heads_in", 4), sems("x_in", 4), sems("out", 4)

    def by_head(ap):
        return ap.rearrange("p (h f) -> p h f", h=HEADS)

    def each_head(ap):
        return ap.unsqueeze(2).to_broadcast([W, HEADS, HID])
    with nc.Block() as block:
        @block.sync
        def _(sp):
            def load(i, c):
                g = group(i, c)
                wait(sp, summed, g - 4 + 1)
                load_group(sp, heads, dram["heads"], heads_in, i, c)
                wait(sp, divided, g - 4 + 1)
                load_group(sp, att, dram["att"][0:z.npad, :], att_in, i, c)

            def load_x(i, c):
                wait(sp, resid, group(i, c) - 4 + 1)
                load_group(sp, xs, dram["x3"], x_in, i, c)

            def store(i, c):
                sp.wait_ge(norm.normed, (group(i, c) + 1) * G)
                x_group(sp, z, result, new, out, i, c, store=True)
            steps(sp, [(12, store), (5, load_x), (0, load)], 0, z.ng, NRING, 1)
            wait_stores(sp, z, out, 16, True)

        @block.gpsimd
        def _(pool):
            def own_loops(i, c):
                g, r = group(i, c), c % 4
                wait_then_step(pool, heads_in[r], loaded_count(z, i, c, 4), pool_step)
                for w in range(G):
                    ex = t["ex_self"][:, bass.ds(g * G + w, 1), :].rearrange("p o h -> p (o h)")
                    ins = pool.tensor_tensor(by_head(heads[:, r, w, 0:HF]), by_head(heads[:, r, w, 0:HF]), each_head(ex), ALU.mult)
                ins.then_inc(owned, 1)

            def bias_x(i, c):
                r = c % 4
                wait_then_step(pool, x_in[r], loaded_count(z, i, c, 4), pool_step)
                pool.tensor_tensor(xs[:, r, :, :], xs[:, r, :, :], wide(wts["L3_fc_b"][0:W, :]), ALU.add).then_inc(x_biased, 1)
            steps(pool, [(9, lambda i, c: norm.power(pool, i, c)), (6, bias_x), (3, own_loops)], 0, z.ng, NRING, 1)

        @block.vector
        def _(dve):
            def add_loops(i, c):
                g, r = group(i, c), c % 4
                dve.wait_ge(att_in[r], loaded_count(z, i, c, 4))
                wait(dve, divided, g - 2 + 1)
                dve.tensor_tensor(den[:, c % 2, :, :], att[:, r, :, HF:HF + HEADS], t["ex_self"][:, bass.ds(g * G, G), :], ALU.add).then_inc(denom, 1)
                dve.wait_ge(owned, g + 1)
                dve.tensor_tensor(att[:, r, :, 0:HF], att[:, r, :, 0:HF], heads[:, r, :, 0:HF], ALU.add).then_inc(summed, 1)
                dve.wait_ge(denom, g + 1)
                dve.reciprocal(den[:, c % 2, :, :], den[:, c % 2, :, :]).then_inc(denom_inv, 1)
                dve.wait_ge(summed, g + 1)
                dve.wait_ge(denom_inv, g + 1)
                wait(dve, turned, g - 4 + 1)
                for w in range(G):
                    ins = dve.tensor_tensor(by_head(mixed[:, r, w, :]), by_head(att[:, r, w, 0:HF]), each_head(den[:, c % 2, w, :]), ALU.mult)
                ins.then_inc(divided, 1)

            def residual(i, c):
                g, r = group(i, c), c % 4
                dve.wait_ge(product, g + 1)
                wait(dve, norm.normed, (g - 4 + 1) * G)
                dve.wait_ge(x_biased, g + 1)
                dve.tensor_tensor(res[:, r, :, :], ps_y[c % 2][:, 0:G, :], xs[:, r, :, :], ALU.add).then_inc(resid, 1)
                dve.wait_ge(resid, g + 1)
                norm.statistics(dve, i, c, res[:, r, :, :])

            def normalize(i, c):
                wait(dve, out[c % 4], uses(i, c, 4) * 16)
                norm.apply(dve, i, c, res[:, c % 4, :, :], new[:, c % 4, :, :])
            steps(dve, [(11, normalize), (8, residual), (4, add_loops)], 0, z.ng, NRING, 1)

        @block.scalar
        def _(act):
            def bias_relu(i, c):
                g = group(i, c)
                act.wait_ge(turned, g + 1)
                wait(act, product, g - 2 + 1)
                for k in range(2):
                    ins = act.activation(relu_t[:, c % 2, k, :, :], ps_t[c % 2][k][:, 0:G, 0:W], ACT.Relu, bias=wts["L3_bias"][:, k:k + 1])
                ins.then_inc(turned_sb, 1)
            steps(act, [(6, bias_relu)], 0, z.ng, NRING, 1)

        @block.tensor
        def _(pe):
            def turn(i, c):
                g = group(i, c)
                pe.wait_ge(divided, g + 1)
                wait(pe, turned_sb, g - 2 + 1)
                for k in range(2):
                    for w in range(G):
                        ins = pe.transpose(ps_t[c % 2][k][:, w, 0:W], mixed[:, c % 4, w, k * D:(k + 1) * D], t["ident"][0:W, 0:W])
                ins.then_inc(turned, 1)

            def multiply(i, c):
                g = group(i, c)
                pe.wait_ge(turned_sb, g + 1)
                wait(pe, resid, g - 2 + 1)
                for w in range(G):
                    for k in range(2):
                        ins = pe.matmul(ps_y[c % 2][:, w, :], relu_t[:, c % 2, k, w, :], wts["L3_fc_w"][:, k * D:(k + 1) * D],
                                        start=(k == 0), stop=(k == 1))
                ins.then_inc(product, 1)
            steps(pe, [(7, multiply), (5, turn)], 0, z.ng, NRING, 1)
    ctx.close()
    sems.close()


_NAMES = ['x', 'src', 'dst', 'L0_gnn_kernel', 'L0_gnn_bias', 'L1_gnn_w_s2d', 'L1_gnn_b_s2d', 'L1_gnn_w_d2s', 'L1_gnn_b_d2s',
          'L1_gnn_w_e1', 'L1_gnn_b_e1', 'L1_gnn_w_e2', 'L1_gnn_b_e2', 'L1_gnn_w_g1', 'L1_gnn_b_g1', 'L1_gnn_w_g2', 'L1_gnn_b_g2',
          'L2_gnn_fc_w', 'L2_gnn_fc_b', 'L2_gnn_f_lw', 'L2_gnn_f_lb', 'L2_gnn_f_rw', 'L2_gnn_n_lw', 'L2_gnn_n_lb', 'L2_gnn_n_rw',
          'L3_gnn_W', 'L3_gnn_att_src', 'L3_gnn_att_dst', 'L3_gnn_bias', 'L3_gnn_fc_w', 'L3_gnn_fc_b']


def gnn_kernel(nc, ins, out, upto=99):
    z = Shapes(ins["x"].shape[0], ins["src"].shape[0])
    assert z.nw <= 512 and z.hi <= HILO and P * z.ns < 1 << 22
    ctx = ExitStack()
    sb = lambda name, shape, dt=FP32: ctx.enter_context(nc.sbuf_tensor(name, shape, dt))
    t = {
        "ident": sb("ident", [P, P]), "iota_win": sb("iota_win", [P, z.nb], FP16), "iota_w": sb("iota_w", [P, W]), "iota_wh": sb("iota_wh", [P, W], FP16),
        "before": sb("before", [P, P], BF16), "after": sb("after", [P, P], BF16),
        "ones": sb("ones", [P, P], BF16), "ones_row": sb("ones_row", [1, P]), "pow": sb("pow", [W, 512]),
        "total": sb("total_slots", [1, 1], I32),
        "keep": sb("keep", [P, 2, z.ns]), "sink": sb("sink", [P, z.ns]),
        "route": sb("route", [97, z.ns], I32),
    }
    for name in ("n_self", "n_self1", "inv_in", "inv_out", "rs_out", "self_w"):
        t[name] = sb(name, [W, z.nw])
    wts, loads = {}, []

    def weight(name, shape, of, to=None):
        wts[name] = sb(f"w_{name}", shape)
        loads.append((wts[name][:, :] if to is None else to(wts[name]), of))

    def rep(name, key):
        v = ins[key]
        if len(v.shape) > 1:
            v = v.rearrange("a b -> (a b)")
        weight(name, [P, v.shape[0]], v.partition_broadcast(P))
    weight("L0_kernel", [P, D], ins["L0_gnn_kernel"])
    rep("L0_bias", "L0_gnn_bias")
    weight("L1_w_e1", [P, 2 * D], ins["L1_gnn_w_e1"].rearrange("(a k) n -> k a n", a=2),
           lambda tile: tile[:, :].rearrange("k (a n) -> k a n", a=2))
    weight("L1_w_g1", [P, 2 * D], ins["L1_gnn_w_g1"].rearrange("(a k) n -> k a n", a=2),
           lambda tile: tile[:, :].rearrange("k (a n) -> k a n", a=2))
    weight("L1_w_s2d", [P, D], ins["L1_gnn_w_s2d"])
    weight("L1_w_d2s", [P, D], ins["L1_gnn_w_d2s"])
    for k in ("b_s2d", "b_d2s", "b_e1", "w_e2", "b_e2", "b_g1", "w_g2", "b_g2"):
        rep(f"L1_{k}", f"L1_gnn_{k}")
    for k in ("fc_w", "f_lw", "f_rw", "n_lw", "n_rw"):
        weight(f"L2_{k}", [P, D], ins[f"L2_gnn_{k}"])
        wts[f"L2_{k}T"] = sb(f"w_L2_{k}T", [P, D])
    for k in ("fc_b", "f_lb", "n_lb"):
        rep(f"L2_{k}", f"L2_gnn_{k}")
    wts["L2_bias"] = sb("w_L2_bias", [P, D])
    weight("L3_W", [P, HF + 2 * HEADS], ins["L3_gnn_W"], lambda tile: tile[:, 0:HF])
    weight("L3_fc_w", [P, 2 * D], ins["L3_gnn_fc_w"].rearrange("(a k) n -> k a n", a=2),
           lambda tile: tile[:, :].rearrange("k (a n) -> k a n", a=2))
    for k in ("att_src", "att_dst", "fc_b"):
        rep(f"L3_{k}", f"L3_gnn_{k}")
    weight("L3_bias", [P, HF // P], ins["L3_gnn_bias"].rearrange("(k p o) -> p k o", p=P, o=1),
           lambda tile: tile[:, :].unsqueeze(2))
    wts["loads"] = loads

    def dr(name, shape, dt=FP32):
        return nc.dram_tensor(name, shape, dt).ap()
    dram = {
        "slots": [dr(f"slots_{k}", [P * z.ns, 2], I32) for k in ("dst", "src")],
        "counts": [dr(f"counts_{k}", [z.nb]) for k in ("dst", "src")],
        "ends": [dr(f"ends_{k}", [-(-z.nw // P) * P]) for k in ("dst", "src")],
        "agg": dr("agg_rows", [z.rows, D]),
        "own": dr("own_rows", [z.npad, 2 * D + 1]), "other": dr("other_rows", [z.npad, 2 * D + 1]),
        "sum_in": dr("sum_in", [z.rows, D + 1]), "sum_out": dr("sum_out", [z.rows, D + 1]),
        "x2": dr("x2_rows", [z.npad, D]), "agg2": dr("agg2_rows", [z.rows, D]),
        "h": dr("h_rows", [z.npad, D]), "agg3": dr("agg3_rows", [z.rows, D]),
        "x3": dr("x3_rows", [z.npad, D]), "heads": dr("heads_rows", [z.npad, HF + HEADS]),
        "a_src": dr("a_src_rows", [z.npad, HEADS]), "shift": dr("shift_rows", [z.npad, 2 * HEADS]),
        "largest": dr("largest", [W, z.nw + 1 + RING, HEADS]), "att": dr("att_rows", [z.rows, HF + HEADS]),
    }
    with ExitStack() as sorting:
        s2 = lambda name, shape, dt=FP32: sorting.enter_context(nc.sbuf_tensor(name, shape, dt))
        t.update(win=s2("win", [P, 2, z.nt]), place=s2("place", [P, 2, z.nt]), carry=s2("carry", [P, z.nt, 2, 2], I32),
                 n_in=s2("n_in", [W, z.nw]), n_out=s2("n_out", [W, z.nw]),
                 self_edge=s2("self_edge", [P, z.nt]), other_edge=s2("other_edge", [P, z.nt]), base=s2("base", [P, 2, z.nb]),
                 att_tmp=s2("att_tmp", [P, HF]))
        load_and_count(nc, z, ins["src"], ins["dst"], t, wts, dram)
        plan_slots(nc, z, t, dram)
        sort_edges(nc, z, t, dram)
    t["slot_tab"] = sb("slot_tab", [P, 2, z.ns, 2], I32)
    t["slot_place"] = sb("slot_place", [P, 2, z.ns])
    load_slots(nc, z, t, dram)
    slot_pass(nc, z, t, "sum0", "rows", 0, ins["x"], dram["agg"])
    dense0(nc, z, t, wts, dram, ins["x"])
    if upto == 0:
        copy_out(nc, z, dram["own"][0:z.n, 0:D], out)
        return
    score = dict(w2=wts["L1_w_e2"][:, :], b2=wts["L1_b_e2"][:, :])
    slot_pass(nc, z, t, "sum1_in", "scored", 0, dram["own"], dram["sum_in"], dram["other"][:, D + 1:2 * D + 1], **score)
    slot_pass(nc, z, t, "sum1_out", "scored", 1, dram["other"], dram["sum_out"], dram["own"][:, D + 1:2 * D + 1], **score)
    dense1(nc, z, t, wts, dram)
    if upto == 1:
        copy_out(nc, z, dram["x2"][0:z.n, 0:D], out)
        return
    slot_pass(nc, z, t, "sum2a", "rows", 0, dram["x2"], dram["agg2"])
    dense2a(nc, z, t, wts, dram)
    slot_pass(nc, z, t, "sum2b", "rows", 0, dram["h"], dram["agg3"])
    t["a_src"], t["a_dst"] = sb("a_src", [W, z.nw, HEADS]), sb("a_dst", [W, z.nw, HEADS])
    dense2b(nc, z, t, wts, dram)
    if upto == 2:
        copy_out(nc, z, dram["x3"][0:z.n, 0:D], out)
        return
    slot_pass(nc, z, t, "max3", "largest", 0, dram["a_src"], dram["largest"])
    t["ex_self"] = sb("ex_self", [W, z.nw, HEADS])
    shifts(nc, z, t, dram)
    slot_pass(nc, z, t, "sum3", "attended", 0, dram["heads"], dram["att"], dram["shift"])
    dense3(nc, z, t, wts, dram, out)


def copy_out(nc, z, of, to):
    s = nc.alloc_semaphore("copied")
    with nc.Block() as block:
        @block.sync
        def _(sp):
            sp.dma_start(to, of).then_inc(s, 16)
            sp.wait_ge(s, 16)


def kernel(**inputs):
    import numpy as _np
    import concourse.bacc as _bacc
    from concourse import mybir as _mybir
    from concourse.bass_utils import run_bass_kernel_spmd as _run

    nc = _bacc.Bacc("TRN2", target_bir_lowering=False, num_devices=1)
    arrays, aps = {}, {}
    for name in _NAMES:
        a = _np.ascontiguousarray(inputs[name])
        arrays[f"in_{name}"] = a
        aps[name] = nc.dram_tensor(f"in_{name}", a.shape, _mybir.dt.from_np(a.dtype), kind="ExternalInput").ap()
    out = nc.dram_tensor("out_0", inputs["x"].shape, _mybir.dt.float32, kind="ExternalOutput").ap()
    gnn_kernel(nc, aps, out)
    r = _run(nc, [arrays], core_ids=[0])
    return r.results[0]["out_0"]
```
